# Optimizing a Trainium2 kernel written in Bass

```python
import numpy as np
import jax
import jax.numpy as jnp

def _softmax(x, axis=-1):
    return jax.nn.softmax(x, axis=axis)

def _gelu(x):
    return jax.nn.gelu(x, approximate=True)

def _silu(x):
    return jax.nn.silu(x)

def _sigmoid(x):
    return jax.nn.sigmoid(x)

def _layernorm(x, axis=-1, eps=1e-05):
    m = jnp.mean(x, axis=axis, keepdims=True)
    v = jnp.var(x, axis=axis, keepdims=True)
    return (x - m) / jnp.sqrt(v + eps)

def _scatter_add(tgt, idx, src, axis=0):
    return tgt.at[idx].add(src)

def _segment_sum(src, seg, n):
    return jax.ops.segment_sum(src, seg, n)
kernel_name = 'mk_prb_d1_jaxref_r8_4991f8'

def setup_inputs(seed: int=0):
    np.random.seed(seed)
    _w = jnp.asarray

    def _L0_attn_setup():
        import jax, jax.numpy as jnp
        import numpy as np
        D = 128
        N = 64
        EPS = 1e-06
        key = jax.random.key(seed)
        ks = jax.random.split(key, 10)
        sD = 1.0 / np.sqrt(D)
        sN = 1.0 / np.sqrt(N)
        x = jax.random.normal(ks[0], (8, 512, D), dtype=jnp.float32)
        A_log = jax.random.normal(ks[1], (N,), dtype=jnp.float32)
        WB = jax.random.uniform(ks[2], (N, D), jnp.float32, -sD, sD)
        bB = jax.random.uniform(ks[3], (N,), jnp.float32, -sD, sD)
        WC = jax.random.uniform(ks[4], (N, D), jnp.float32, -sD, sD)
        bC = jax.random.uniform(ks[5], (N,), jnp.float32, -sD, sD)
        Wd = jax.random.uniform(ks[6], (1, D), jnp.float32, -sD, sD)
        bd = jax.random.uniform(ks[7], (1,), jnp.float32, -sD, sD)
        Wo = jax.random.uniform(ks[8], (D, N), jnp.float32, -sN, sN)
        bo = jax.random.uniform(ks[9], (D,), jnp.float32, -sN, sN)
        return {'x': x, 'A_log': A_log, 'WB': WB, 'bB': bB, 'WC': WC, 'bC': bC, 'Wd': Wd, 'bd': bd, 'Wo': Wo, 'bo': bo}
    _L0_attn_in = _L0_attn_setup()

    def _L0_ffn_setup():
        import jax, jax.numpy as jnp
        import numpy as np
        from jax import lax
        DIM = 128
        INTER = 64
        N_EXPERTS = 16
        TOPK = 4
        ROUTE_SCALE = 2.5
        VOCAB = 4000

        def _silu_and_mul(gu):
            gate, up = jnp.split(gu, 2, axis=-1)
            return jax.nn.silu(gate) * up
        key = jax.random.key(seed)
        ks = jax.random.split(key, 8)
        x = jax.random.normal(ks[0], (2, 64, DIM), dtype=jnp.float32)
        input_ids = jax.random.randint(ks[1], (2, 64), 0, VOCAB)
        s = 0.02
        gate_w = jax.random.normal(ks[2], (N_EXPERTS, DIM), dtype=jnp.float32) * s
        gate_b = jax.random.normal(ks[3], (N_EXPERTS,), dtype=jnp.float32) * s
        w13 = jax.random.normal(ks[4], (N_EXPERTS, 2 * INTER, DIM), dtype=jnp.float32) * s
        w2 = jax.random.normal(ks[5], (N_EXPERTS, DIM, INTER), dtype=jnp.float32) * s
        w13_s = jax.random.normal(ks[6], (2 * INTER, DIM), dtype=jnp.float32) * s
        w2_s = jax.random.normal(ks[7], (DIM, INTER), dtype=jnp.float32) * s
        return {'x': x, 'input_ids': input_ids, 'gate_w': gate_w, 'gate_b': gate_b, 'w13': w13, 'w2': w2, 'w13_s': w13_s, 'w2_s': w2_s}
    _L0_ffn_in = _L0_ffn_setup()
    _d = {'L0_attn_x': _L0_attn_in['x'], 'L0_attn_A_log': _L0_attn_in['A_log'], 'L0_attn_WB': _L0_attn_in['WB'], 'L0_attn_bB': _L0_attn_in['bB'], 'L0_attn_WC': _L0_attn_in['WC'], 'L0_attn_bC': _L0_attn_in['bC'], 'L0_attn_Wd': _L0_attn_in['Wd'], 'L0_attn_bd': _L0_attn_in['bd'], 'L0_attn_Wo': _L0_attn_in['Wo'], 'L0_attn_bo': _L0_attn_in['bo'], 'L0_ffn_input_ids': _L0_ffn_in['input_ids'], 'L0_ffn_gate_w': _L0_ffn_in['gate_w'], 'L0_ffn_gate_b': _L0_ffn_in['gate_b'], 'L0_ffn_w13': _L0_ffn_in['w13'], 'L0_ffn_w2': _L0_ffn_in['w2'], 'L0_ffn_w13_s': _L0_ffn_in['w13_s'], 'L0_ffn_w2_s': _L0_ffn_in['w2_s']}
    _x0 = _d['L0_attn_x']
    _d['L0_attn_x'] = jax.random.normal(jax.random.fold_in(jax.random.key(seed), 1), (4, 512, 128), dtype=_x0.dtype)
    del _x0
    return _d

def reference(L0_attn_x, L0_attn_A_log, L0_attn_WB, L0_attn_bB, L0_attn_WC, L0_attn_bC, L0_attn_Wd, L0_attn_bd, L0_attn_Wo, L0_attn_bo, L0_ffn_input_ids, L0_ffn_gate_w, L0_ffn_gate_b, L0_ffn_w13, L0_ffn_w2, L0_ffn_w13_s, L0_ffn_w2_s):

    def _L0_attn_ref(x, A_log, WB, bB, WC, bC, Wd, bd, Wo, bo):
        import jax, jax.numpy as jnp
        import numpy as np
        D = 128
        N = 64
        EPS = 1e-06
        A = -jax.nn.softplus(A_log)
        B_t = jnp.einsum('bld,nd->bln', x, WB) + bB
        _C_proj = jnp.einsum('bld,nd->bln', x, WC) + bC
        Delta = jax.nn.softplus(jnp.einsum('bld,nd->bln', x, Wd) + bd)
        dA = jnp.exp(A * Delta)
        dB = (dA - 1.0) / (A + EPS) * B_t
        conv = jnp.cumprod(dA, axis=1)
        ones = jnp.ones_like(dA[:, :1, :])
        Ct = jnp.concatenate([ones, conv[:, :-1, :]], axis=1)
        z = dB / (Ct + EPS)
        s = jnp.cumsum(z, axis=1)
        X_state = Ct * s
        Y = jnp.einsum('bln,dn->bld', Ct * X_state, Wo) + bo
        return Y

    def _L0_ffn_ref(x, input_ids, gate_w, gate_b, w13, w2, w13_s, w2_s):
        import jax, jax.numpy as jnp
        import numpy as np
        from jax import lax
        DIM = 128
        INTER = 64
        N_EXPERTS = 16
        TOPK = 4
        ROUTE_SCALE = 2.5
        VOCAB = 4000

        def _silu_and_mul(gu):
            gate, up = jnp.split(gu, 2, axis=-1)
            return jax.nn.silu(gate) * up
        B, S, D = x.shape
        xt = x.reshape(-1, D)
        T = xt.shape[0]
        scores = jax.nn.sigmoid(xt.astype(jnp.float32) @ gate_w.T)
        biased = scores + gate_b
        _, idx = lax.top_k(biased, TOPK)
        w = jnp.take_along_axis(scores, idx, axis=-1)
        w = w / jnp.sum(w, axis=-1, keepdims=True)
        w = w * ROUTE_SCALE
        comb = jnp.zeros((T, N_EXPERTS), jnp.float32)
        comb = comb.at[jnp.arange(T)[:, None], idx].add(w)
        comb = comb.astype(x.dtype)

        def expert_body(y, args):
            w13_e, w2_e, c_e = args
            h = _silu_and_mul(xt @ w13_e.T)
            return (y + c_e[:, None] * (h @ w2_e.T), None)
        y, _ = lax.scan(expert_body, jnp.zeros_like(xt), (w13, w2, comb.T))
        y = y + _silu_and_mul(xt @ w13_s.T) @ w2_s.T
        return y.astype(x.dtype).reshape(B, S, D)
    x = L0_attn_x
    xn = _layernorm(x, axis=-1)
    x = x + _L0_attn_ref(xn, L0_attn_A_log, L0_attn_WB, L0_attn_bB, L0_attn_WC, L0_attn_bC, L0_attn_Wd, L0_attn_bd, L0_attn_Wo, L0_attn_bo) + _L0_ffn_ref(xn, L0_ffn_input_ids, L0_ffn_gate_w, L0_ffn_gate_b, L0_ffn_w13, L0_ffn_w2, L0_ffn_w13_s, L0_ffn_w2_s)
    return x

_drawn_inputs = setup_inputs


def setup_inputs(seed=0):
    import zlib

    import numpy as np

    out = dict(_drawn_inputs(seed))
    spreads = {}
    factors = {'L0_attn_A_log': 3.142,
     'L0_attn_bB': 8.0,
     'L0_attn_Wd': 5.953,
     'L0_ffn_gate_w': 8.0,
     'L0_ffn_gate_b': 8.0,
     'L0_ffn_w13': 8.0,
     'L0_ffn_w2': 8.0,
     'L0_ffn_w13_s': 8.0,
     'L0_ffn_w2_s': 8.0,
     'L0_attn_bo': 8.0}
    for name, (base, spread) in spreads.items():
        noise = np.random.default_rng([zlib.crc32(name.encode()), seed]).standard_normal(out[name].shape)
        drawn = base * np.exp(spread * noise) if base else spread * noise
        out[name] = jnp.asarray(drawn.astype(out[name].dtype))
    for name, factor in factors.items():
        out[name] = (out[name] * factor).astype(out[name].dtype)
    return out
```

```python
from contextlib import ExitStack

import numpy as np

import concourse.bass as bass
from concourse import mybir

F32 = mybir.dt.float32
F32R = mybir.dt.float32r
BF16 = mybir.dt.bfloat16
ALU = mybir.AluOpType
ACT = mybir.ActivationFunctionType
AX_X = mybir.AxisListType.X

P = 128
BATCH, SEQ, D = 4, 512, 128
STATES = 64
EXPERTS, INTER, TOPK = 16, 64, 4
ROUTE_SCALE = 2.5
ATTN_EPS, LN_EPS = 1e-6, 1e-5

TILE = SEQ
TILES = BATCH
SUB = TILE // P
BLOCKS = TILES * SUB
PAIRS = EXPERTS // 2
STEPS = PAIRS + 1
GROUPS = BATCH // 2
ROUTE = EXPERTS + 2
PARTS = 3
ROW = EXPERTS + 1
KSEL = PARTS * ROW
TAKEN = -3.0e38
FILLER = -2.0e38
WIDE = EXPERTS + 8 - TOPK

C_ROUTE = 0
C_UP = C_ROUTE + ROUTE
C_SHARED = C_UP + PAIRS * 256
C_B = C_SHARED + 256
C_DOWN = C_B + 256
C_TAIL = C_DOWN + PAIRS * 128
C_END = C_TAIL + 256
LOADS = [(0, C_UP + 256), (C_UP + 256, C_UP + 4 * 256), (C_UP + 4 * 256, C_DOWN), (C_DOWN, C_END)]
PIECES = [(0, C_UP + 256)] + [(C_UP + 256 * e, C_UP + 256 * (e + 1)) for e in range(1, PAIRS)] + [
    (C_SHARED, C_DOWN), (C_DOWN, C_DOWN + 512), (C_DOWN + 512, C_TAIL), (C_TAIL, C_END)]
V_ALOG, V_BB, V_BO, V_BD, V_GB = 0, 1, 2, 3, 4
V_END = V_GB + EXPERTS
SELECTORS = PAIRS + 2

SILU_BUFS = 3
V_BUFS = 14
H_BUFS = 3
SPLIT_BUFS = 4
LEAD = 2


def piece_of(column):
    return next(n for n, (a, b) in enumerate(PIECES) if a <= column < b)


def load_of(piece):
    return next(n for n, (a, b) in enumerate(LOADS) if a <= PIECES[piece][0] < b)


def make_plan():
    plan = [("stats", 0), ("split", 0), ("norm", 0), ("stats", 1), ("turn", 0), ("split", 1), ("stats", 2),
            ("up", 0), ("stats", 3), ("split", 2), ("norm", 1), ("up", 1), ("split", 3), ("turn", 1), ("norm", 2),
            ("logits", 0), ("up", 2), ("split", 4), ("norm", 3), ("turn", 2), ("logits", 1), ("up", 3), ("turn", 3),
            ("split", 5), ("split", 6), ("logits", 2), ("up", 4), ("logits", 3), ("up", 5), ("split", 7), ("consts", 0),
            ("route", 0), ("up", 6), ("route", 1), ("up", 7), ("route", 2), ("split", 8), ("up", 8), ("route", 3),
            ("up", 9), ("route", 4), ("split", 9), ("up", 10), ("route", 5), ("split", 10), ("split", 11),
            ("spread", 0)]
    attention = [[("delta", 0), ("delta", 1), ("decay", 0), ("bproj", 0), ("bproj", 1), ("attn", 0)]]
    attention += [[("attn", 1), ("attn", 2), ("attn", 3)], [("attn", 4), ("attn", 5), ("attn", 6)],
                  [("attn", 7)], [("attn", 8)]]
    attention += [[("attn", 10 + n)] for n in range(9)]
    down, cast = 0, 0
    total = TILES * STEPS
    for j in range(11, total + 1):
        if j < total:
            plan.append(("up", j))
        if attention:
            plan += attention.pop(0)
        upto = min(j - LEAD, (j - 10) * total // (total - 11)) if j < total else total
        while down < upto:
            while cast < min(total, down + 1 + LEAD) and (cast < j or j == total):
                plan.append(("cast", cast))
                cast += 1
            plan.append(("down", down))
            if down % STEPS == STEPS - 1:
                plan.append(("out", down // STEPS))
            down += 1
    assert not attention
    assert plan.index(("attn", 8)) < plan.index(("cast", 8)) and plan.index(("attn", 18)) < plan.index(("cast", 26))
    order = [x for x in plan if x[0] in ("up", "cast") and x[1] % STEPS < PAIRS]
    for n, (what, k) in enumerate(order):
        if what == "up":
            ahead = sum(1 for w_, _ in order[:n] if w_ == "up") - sum(1 for w_, _ in order[:n] if w_ == "cast")
            assert ahead < V_BUFS
    return plan


def build(nc, x_rows, x_cols, weights, vectors, sel, ident, out):
    plan = make_plan()
    with ExitStack() as ctx:
        def sb(name, shape, dt=F32):
            return ctx.enter_context(nc.sbuf_tensor(name, shape, dt))

        def sem(name):
            return ctx.enter_context(nc.semaphore(name))

        xr = sb("xr", [P, BLOCKS, D])
        xt = sb("xt", [P, BATCH * SEQ])
        w = sb("w", [P, C_END])
        wh = sb("wh", [P, C_END], F32R)
        wl = sb("wl", [P, C_END], F32R)
        vec = sb("vec", [P, V_END])
        sels = sb("sels", [KSEL, SELECTORS, P], BF16)
        idf = sb("idf", [P, P])
        idb = sb("idb", [P, P], BF16)
        stats = sb("stats", [P, BLOCKS, 6])
        moments = sb("moments", [P, BLOCKS, 2])
        var_eps = sb("var_eps", [P, BLOCKS])
        neg_mean = sb("neg_mean", [P, BLOCKS])
        minus_half = sb("minus_half", [P, SUB])
        rstd = sb("rstd", [P, BLOCKS])
        xn = sb("xn", [P, BLOCKS, D])
        xh = sb("xh", [P, BATCH * SEQ], F32R)
        xl = sb("xl", [P, BATCH * SEQ], F32R)
        zb = sb("zb", [P, BLOCKS + 1])
        zabs = sb("zabs", [P, BLOCKS + 1])
        zexp = sb("zexp", [P, BLOCKS + 1])
        zexp1 = sb("zexp1", [P, BLOCKS + 1])
        zexp1_rec = sb("zexp1_rec", [P, BLOCKS + 1])
        zlost = sb("zlost", [P, BLOCKS + 1])
        zfix = sb("zfix", [P, BLOCKS + 1])
        zln = sb("zln", [P, BLOCKS + 1])
        zlog1p = sb("zlog1p", [P, BLOCKS + 1])
        softplus = sb("softplus", [P, BLOCKS + 1])
        a_neg = sb("a_neg", [P, 1])
        a_eps = sb("a_eps", [P, 1])
        a_rec = sb("a_rec", [P, 1])
        bb_rec = sb("bb_rec", [P, 1])
        lexp = sb("lexp", [P, BLOCKS, EXPERTS])
        lexp1 = sb("lexp1", [P, BLOCKS, EXPERTS])
        scores = sb("scores", [P, BLOCKS, EXPERTS])
        biased = sb("biased", [P, BLOCKS, WIDE])
        top8 = sb("top8", [P, BLOCKS, 8])
        marked = sb("marked", [P, BLOCKS, WIDE])
        chosen = sb("chosen", [P, BLOCKS, EXPERTS])
        picked = sb("picked", [P, BLOCKS, EXPERTS])
        total = sb("total", [P, BLOCKS])
        total_rec = sb("total_rec", [P, BLOCKS])
        routed = sb("routed", [P, BLOCKS, ROW])
        rest1 = sb("rest1", [P, BLOCKS, ROW])
        rest2 = sb("rest2", [P, BLOCKS, ROW])
        routed16 = sb("routed16", [P, BLOCKS, PARTS, ROW], BF16)
        routed_t = sb("routed_t", [KSEL, BATCH * SEQ], BF16)
        silu = sb("silu", [P, SILU_BUFS, TILE])
        v = sb("v", [P, V_BUFS, TILE])
        h = sb("h", [P, H_BUFS, TILE])
        hh = sb("hh", [P, SPLIT_BUFS, TILE], F32R)
        hl = sb("hl", [P, SPLIT_BUFS, TILE], F32R)
        tail = sb("tail", [P, TILES, TILE])
        sels_in = tail[0:KSEL, 0:3, :].rearrange("k t n -> k (t n)")[:, 0:SELECTORS * P].rearrange(
            "k (s n) -> k s n", s=SELECTORS)
        ones = sb("ones", [P, TILE])
        zeros = sb("zeros", [P, TILE])
        da = sb("da", [P, GROUPS, TILE])
        ct = sb("ct", [P, GROUPS, TILE + 1])
        ct_eps = sb("ct_eps", [P, GROUPS, TILE])
        ct_rec = sb("ct_rec", [P, GROUPS, TILE])
        bs = sb("bs", [P, GROUPS, TILE])
        db = sb("db", [P, GROUPS, TILE])
        z, s, state = ct_eps, da, bs
        y = sb("y", [P, 2, TILE])

        def bank(name):
            return ctx.enter_context(nc.psum_tensor(name, [P, TILE], F32))

        gate_ps = [bank("gate0"), bank("gate1")]
        up_ps = [bank("up0"), bank("up1")]
        cast_ps = bank("cast")
        y_ps = [bank("y0"), bank("y1")]
        misc_ps = bank("misc")
        turn_ps = [y_ps[0], y_ps[1], cast_ps, y_ps[0]]
        logits = misc_ps[:, 0:BLOCKS * ROUTE].rearrange("p (q r) -> p q r", r=ROUTE)
        spread_ps = [y_ps[1], misc_ps]
        pair_ps = [y_ps[1], misc_ps]

        consts_done = sem("consts_done")
        x_in = [sem(f"x_in{b}") for b in range(TILES)]
        w_in = [sem(f"w_in{n}") for n in range(len(LOADS))]
        const_in = sem("const_in")
        xt_in = sem("xt_in")
        filled = sem("filled")
        var_done = sem("var_done")
        rstd_done = sem("rstd_done")
        norm_done = sem("norm_done")
        norm_pool = sem("norm_pool")
        turned = sem("turned")
        xh_done = sem("xh_done")
        xl_done = sem("xl_done")
        wh_done = sem("wh_done")
        wl_done = sem("wl_done")
        logits_done = sem("logits_done")
        zb_done = sem("zb_done")
        exp_done = sem("exp_done")
        act_step = sem("act_step")
        dve_step = sem("dve_step")
        pool_step = sem("pool_step")
        routed_done = sem("routed_done")
        spread_done = sem("spread_done")
        routed_t_done = sem("routed_t_done")
        delta_done = sem("delta_done")
        da_done = sem("da_done")
        b_done = sem("b_done")
        bs_done = sem("bs_done")
        ct_done = sem("ct_done")
        ct_eps_done = sem("ct_eps_done")
        db_done = sem("db_done")
        rec_done = sem("rec_done")
        z_done = sem("z_done")
        s_done = sem("s_done")
        state_done = sem("state_done")
        attn_done = sem("attn_done")
        up_done = sem("up_done")
        silu_done = sem("silu_done")
        v_done = sem("v_done")
        cast_done = sem("cast_done")
        h_done = sem("h_done")
        hh_done = sem("hh_done")
        hl_done = sem("hl_done")
        down_done = sem("down_done")
        y_done = sem("y_done")
        y_out = [sem("y_out0"), sem("y_out1")]

        block = ctx.enter_context(nc.Block())

        def pairs_before(k):
            return k // STEPS * PAIRS + min(k % STEPS, PAIRS)

        def cols(b):
            return slice(b * TILE, (b + 1) * TILE)

        def shared_half(b):
            return slice(64, 128) if b % 2 == 0 else slice(0, 64)

        def attn_half(b):
            return slice(0, 64) if b % 2 == 0 else slice(64, 128)

        @block.sync
        def _(sp):
            sp.dma_start(xr[:, 0:SUB, :], x_rows[:, 0:SUB, :]).then_inc(x_in[0], 16)
            for b in range(1, TILES):
                sp.dma_start(xr[:, b * SUB:(b + 1) * SUB, :],
                             x_rows[:, b * SUB:(b + 1) * SUB, :]).then_inc(x_in[b], 16)
                if b == 1:
                    sp.dma_start(vec[:], vectors).then_inc(const_in, 16)
                    sp.dma_start(sels_in, sel).then_inc(const_in, 16)
            sp.dma_start(xt[:], x_cols).then_inc(xt_in, 16)
            for b in range(TILES):
                sp.wait_ge(y_done, b + 1)
                sp.dma_start(out[:, cols(b)], y[:, b % 2, :]).then_inc(y_out[b % 2], 16)
            for n in range(2):
                sp.wait_ge(y_out[n], 16 * TILES // 2)

        @block.gpsimd
        def _(pool):
            steps = [0]

            def link(ins):
                steps[0] += 1
                ins.then_inc(pool_step, 1)
                pool.wait_ge(pool_step, steps[0])

            pool.memset(minus_half[:], -0.5).then_inc(filled, 1)
            pool.memset(ones[:], 1.0).then_inc(filled, 1)
            pool.memset(zeros[:], 0.0).then_inc(filled, 1)
            pool.memset(ct[:, :, 0:1], 1.0).then_inc(filled, 1)
            pool.memset(biased[:, :, EXPERTS:WIDE], FILLER).then_inc(filled, 1)
            pool.wait_ge(filled, 5)
            for what, n in plan:
                if what == "stats":
                    q = slice(n * SUB, (n + 1) * SUB)
                    pool.wait_ge(var_done, n + 1)
                    pool.tensor_tensor(rstd[:, q], var_eps[:, q], minus_half[:], ALU.pow).then_inc(rstd_done, 1)
                if what == "norm" and n > 0:
                    pool.wait_ge(rstd_done, n + 1)
                    for q in range(n * SUB, (n + 1) * SUB):
                        last = pool.tensor_scalar(xn[:, q, :], xr[:, q, :], neg_mean[:, q:q + 1],
                                                  rstd[:, q:q + 1], ALU.add, ALU.mult)
                    last.then_inc(norm_pool, 1)
                if what == "split":
                    a, b = PIECES[n]
                    pool.wait_ge(wh_done, n + 1)
                    pool.tensor_tensor(wl[:, a:b], w[:, a:b], wh[:, a:b].bitcast(F32),
                                       ALU.subtract).then_inc(wl_done, 1)
                if what == "attn" and n % 10 == 1:
                    g = n // 10
                    pool.wait_ge(ct_done, g + 1)
                    pool.tensor_scalar(ct_eps[:, g, :], ct[:, g, 0:TILE], ATTN_EPS, 1.0, ALU.add,
                                       ALU.mult).then_inc(ct_eps_done, 1)
                if what == "attn" and n % 10 == 6:
                    g = n // 10
                    pool.wait_ge(rec_done, 4 * (g + 1))
                    pool.wait_ge(db_done, g + 1)
                    pool.tensor_tensor(z[:, g, :], db[:, g, :], ct_rec[:, g, :], ALU.mult).then_inc(z_done, 1)
                if what == "attn" and n % 10 == 7:
                    g = n // 10
                    pool.wait_ge(s_done, g + 1)
                    pool.tensor_tensor(state[:, g, :], ct[:, g, 0:TILE], s[:, g, :],
                                       ALU.mult).then_inc(state_done, 1)
                if what == "cast":
                    b, e = divmod(n, STEPS)
                    pool.wait_ge(hh_done, n + 1)
                    if n >= SPLIT_BUFS:
                        pool.wait_ge(down_done, n - SPLIT_BUFS + 1)
                    src = h[:, pairs_before(n) % H_BUFS, :] if e < PAIRS else tail[:, b, :]
                    pool.tensor_tensor(hl[:, n % SPLIT_BUFS, :], src, hh[:, n % SPLIT_BUFS, :].bitcast(F32),
                                       ALU.subtract).then_inc(hl_done, 1)

        @block.scalar
        def _(act):
            steps = [0]

            def link(ins):
                steps[0] += 1
                ins.then_inc(act_step, 1)
                act.wait_ge(act_step, steps[0])

            for n, (a, b) in enumerate(LOADS):
                act.dma_start(w[:, a:b], weights[:, a:b]).then_inc(w_in[n], 16)
                if n == 0:
                    act.dma_start(idf[:], ident).then_inc(const_in, 16)
            act.preload_act_table_set("silu_and_others")
            for what, n in plan:
                if what == "split":
                    a, b = PIECES[n]
                    act.wait_ge(w_in[load_of(n)], 16)
                    act.activation(wh[:, a:b], w[:, a:b], ACT.Copy).then_inc(wh_done, 1)
                if what == "consts":
                    act.wait_ge(const_in, 48)
                    act.activation(sels[:], sels_in, ACT.Copy).then_inc(consts_done, 1)
                    act.activation(idb[:], idf[:], ACT.Copy).then_inc(consts_done, 1)
                if what == "turn":
                    act.wait_ge(turned, n + 1)
                    act.activation(xh[:, cols(n)], turn_ps[n][:], ACT.Copy).then_inc(xh_done, 1)
                if what == "route" and n == 0:
                    act.preload_act_table_set("natural_log_exp_and_others")
                    act.wait_ge(zb_done, 1)
                    act.activation(lexp[:], logits[:, :, 0:EXPERTS], ACT.Exp, scale=-1.0).then_inc(exp_done, 1)
                    link(act.activation(zabs[:], zb[:], ACT.Abs))
                    link(act.activation(zexp[:], zabs[:], ACT.Exp, scale=-1.0))
                    act.activation(zln[:], zexp[:], ACT.Ln, bias=1.0).then_inc(exp_done, 1)
                    act.preload_act_table_set("silu_and_others")
                if what == "spread":
                    for m in range(2):
                        act.wait_ge(spread_done, m + 1)
                        act.activation(routed_t[:, 2 * m * TILE:(2 * m + 2) * TILE],
                                       spread_ps[m][:].bitcast(BF16)[0:KSEL, :], ACT.Copy).then_inc(routed_t_done, 1)
                if what == "decay":
                    act.preload_act_table_set("natural_log_exp_and_others")
                    act.wait_ge(routed_done, 2)
                    for g in range(GROUPS):
                        act.wait_ge(delta_done, g + 1)
                        act.activation(da[:, g, :], pair_ps[g][:], ACT.Exp, scale=a_neg[:, 0:1]).then_inc(da_done, 1)
                    act.preload_act_table_set("silu_and_others")
                if what == "bproj":
                    act.wait_ge(b_done, n + 1)
                    act.activation(bs[:, n, :], pair_ps[n][:], ACT.Identity, bias=bb_rec[:, 0:1],
                                   scale=a_rec[:, 0:1]).then_inc(bs_done, 1)
                if what == "up":
                    b, e = divmod(n, STEPS)
                    act.wait_ge(up_done, n + 1)
                    if n >= SILU_BUFS:
                        act.wait_ge(v_done, n - SILU_BUFS + 1)
                    if e < PAIRS:
                        act.activation(silu[:, n % SILU_BUFS, :], gate_ps[n % 2][:], ACT.Silu).then_inc(silu_done, 1)
                    else:
                        act.activation(silu[shared_half(b), n % SILU_BUFS, :], gate_ps[n % 2][attn_half(b), :],
                                       ACT.Silu).then_inc(silu_done, 1)
                if what == "cast":
                    b, e = divmod(n, STEPS)
                    if e < PAIRS:
                        act.wait_ge(h_done, pairs_before(n) + 1)
                    else:
                        act.wait_ge(v_done, n + 1)
                        act.wait_ge(attn_done, b + 1)
                    if n >= SPLIT_BUFS:
                        act.wait_ge(down_done, n - SPLIT_BUFS + 1)
                    src = h[:, pairs_before(n) % H_BUFS, :] if e < PAIRS else tail[:, b, :]
                    act.activation(hh[:, n % SPLIT_BUFS, :], src, ACT.Copy).then_inc(hh_done, 1)

        @block.vector
        def _(dve):
            steps = [0]

            def link(ins):
                steps[0] += 1
                ins.then_inc(dve_step, 1)
                dve.wait_ge(dve_step, steps[0])

            for what, n in plan:
                if what == "stats":
                    dve.wait_ge(x_in[n], 16)
                    qs = range(n * SUB, (n + 1) * SUB)
                    for q in qs:
                        last = dve.bn_stats(stats[:, q, :], xr[:, q, :])
                    link(last)
                    for q in qs:
                        last = dve.bn_aggr(moments[:, q, :], stats[:, q, :])
                    link(last)
                    dve.tensor_scalar(neg_mean[:, qs.start:qs.stop], moments[:, qs.start:qs.stop, 0], -1.0, None,
                                      ALU.mult)
                    dve.tensor_scalar(var_eps[:, qs.start:qs.stop], moments[:, qs.start:qs.stop, 1], LN_EPS, None,
                                      ALU.add).then_inc(var_done, 1)
                if what == "norm" and n == 0:
                    dve.wait_ge(rstd_done, 1)
                    dve.wait_ge(var_done, 1)
                    for q in range(SUB):
                        last = dve.tensor_scalar(xn[:, q, :], xr[:, q, :], neg_mean[:, q:q + 1],
                                                 rstd[:, q:q + 1], ALU.add, ALU.mult)
                    last.then_inc(norm_done, 1)
                if what == "turn":
                    dve.wait_ge(xh_done, n + 1)
                    dve.tensor_tensor(xl[:, cols(n)], turn_ps[n][:], xh[:, cols(n)].bitcast(F32),
                                      ALU.subtract).then_inc(xl_done, 1)
                if what == "route" and n == 0:
                    dve.wait_ge(const_in, 48)
                    dve.wait_ge(logits_done, TILES)
                    dve.wait_ge(filled, 5)
                    dve.tensor_copy(zb[:, BLOCKS:BLOCKS + 1], vec[:, V_ALOG:V_ALOG + 1])
                    dve.tensor_scalar(zb[:, 0:BLOCKS], logits[:, :, EXPERTS], vec[:, V_BD:V_BD + 1], None,
                                      ALU.add).then_inc(zb_done, 1)
                if what == "route" and n == 1:
                    dve.wait_ge(exp_done, 1)
                    link(dve.tensor_scalar(lexp1[:], lexp[:], 1.0, None, ALU.add))
                    link(dve.reciprocal(scores[:], lexp1[:]))
                    link(dve.tensor_tensor(biased[:, :, 0:EXPERTS], scores[:],
                                           vec[:, None, V_GB:V_END].to_broadcast([P, BLOCKS, EXPERTS]), ALU.add))
                if what == "route" and n == 2:
                    for q in range(BLOCKS):
                        last = dve.max(top8[:, q, :], biased[:, q, 0:EXPERTS])
                    link(last)
                    link(dve.memset(top8[:, :, TOPK:8], FILLER))
                if what == "route" and n == 3:
                    for q in range(BLOCKS):
                        last = dve.match_replace(marked[:, q, :], top8[:, q, :], biased[:, q, :], TAKEN)
                    link(last)
                    link(dve.tensor_tensor(chosen[:], marked[:, :, 0:EXPERTS], biased[:, :, 0:EXPERTS],
                                           ALU.not_equal))
                if what == "route" and n == 4:
                    link(dve.tensor_tensor(picked[:], scores[:], chosen[:], ALU.mult))
                    link(dve.tensor_reduce(total[:], picked[:], AX_X, ALU.add))
                    link(dve.reciprocal(total_rec[:], total[:]))
                    link(dve.scalar_tensor_tensor(out=routed[:, :, 0:EXPERTS], in0=picked[:], scalar=ROUTE_SCALE,
                                                  in1=total_rec[:, :, None].to_broadcast([P, BLOCKS, EXPERTS]),
                                                  op0=ALU.mult, op1=ALU.mult))
                    dve.wait_ge(exp_done, 2)
                    link(dve.tensor_scalar(zexp1[:], zexp[:], 1.0, None, ALU.add))
                    link(dve.scalar_tensor_tensor(out=zlost[:], in0=zexp1[:], scalar=1.0, in1=zexp[:],
                                                  op0=ALU.subtract, op1=ALU.subtract))
                    link(dve.reciprocal(zexp1_rec[:], zexp1[:]))
                    link(dve.tensor_tensor(zfix[:], zlost[:], zexp1_rec[:], ALU.mult))
                    link(dve.tensor_tensor(zlog1p[:], zln[:], zfix[:], ALU.subtract))
                    link(dve.scalar_tensor_tensor(out=softplus[:], in0=zb[:], scalar=0.0, in1=zlog1p[:], op0=ALU.max,
                                                  op1=ALU.add))
                    link(dve.tensor_copy(routed[:, :, EXPERTS], softplus[:, 0:BLOCKS]))
                if what == "route" and n == 5:
                    link(dve.tensor_copy(routed16[:, :, 0, :], routed[:]))
                    link(dve.tensor_tensor(rest1[:], routed[:], routed16[:, :, 0, :], ALU.subtract))
                    link(dve.tensor_copy(routed16[:, :, 1, :], rest1[:]))
                    link(dve.tensor_tensor(rest2[:], rest1[:], routed16[:, :, 1, :], ALU.subtract))
                    dve.tensor_copy(routed16[:, :, 2, :], rest2[:]).then_inc(routed_done, 1)
                    link(dve.tensor_scalar(a_neg[:], softplus[:, BLOCKS:BLOCKS + 1], -1.0, None, ALU.mult))
                    link(dve.tensor_scalar(a_eps[:], a_neg[:], ATTN_EPS, None, ALU.add))
                    link(dve.reciprocal(a_rec[:], a_eps[:]))
                    dve.tensor_tensor(bb_rec[:], vec[:, V_BB:V_BB + 1], a_rec[:], ALU.mult).then_inc(routed_done, 1)
                if what == "attn":
                    g, part = divmod(n, 10)
                    if part == 0:
                        dve.wait_ge(da_done, g + 1)
                        dve.tensor_tensor_scan(ct[:, g, 1:TILE + 1], da[:, g, :], zeros[:], 1.0, ALU.mult,
                                               ALU.add).then_inc(ct_done, 1)
                    if part == 1:
                        dve.wait_ge(bs_done, g + 1)
                        dve.scalar_tensor_tensor(out=db[:, g, :], in0=da[:, g, :], scalar=1.0, in1=bs[:, g, :],
                                                 op0=ALU.subtract, op1=ALU.mult).then_inc(db_done, 1)
                    if 2 <= part < 6:
                        c = slice((part - 2) * P, (part - 1) * P)
                        dve.wait_ge(ct_eps_done, g + 1)
                        dve.reciprocal(ct_rec[:, g, c], ct_eps[:, g, c]).then_inc(rec_done, 1)
                    if part == 7:
                        dve.wait_ge(z_done, g + 1)
                        dve.tensor_tensor_scan(s[:, g, :], ones[:], z[:, g, :], 0.0, ALU.mult,
                                               ALU.add).then_inc(s_done, 1)
                    if part == 8:
                        dve.wait_ge(state_done, g + 1)
                        for b in (2 * g, 2 * g + 1):
                            half = attn_half(b)
                            dve.wait_ge(consts_done, 1)
                            dve.tensor_tensor(tail[half, b, :], ct[half, g, 0:TILE], state[half, g, :],
                                              ALU.mult).then_inc(attn_done, 1)
                if what == "up":
                    b, e = divmod(n, STEPS)
                    dve.wait_ge(silu_done, n + 1)
                    if e < PAIRS:
                        dve.tensor_tensor(v[:, pairs_before(n) % V_BUFS, :], silu[:, n % SILU_BUFS, :],
                                          up_ps[n % 2][:], ALU.mult).then_inc(v_done, 1)
                    else:
                        half = shared_half(b)
                        dve.wait_ge(consts_done, 1)
                        dve.tensor_tensor(tail[half, b, :], silu[half, n % SILU_BUFS, :], gate_ps[n % 2][half, :],
                                          ALU.mult).then_inc(v_done, 1)
                if what == "cast" and n % STEPS < PAIRS:
                    i = pairs_before(n)
                    dve.wait_ge(cast_done, i + 1)
                    dve.wait_ge(v_done, n + 1)
                    if i >= H_BUFS:
                        k = next(k for k in range(n) if pairs_before(k) == i - H_BUFS and k % STEPS < PAIRS)
                        dve.wait_ge(hl_done, k + 1)
                    dve.tensor_tensor(h[:, i % H_BUFS, :], v[:, i % V_BUFS, :], cast_ps[:],
                                      ALU.mult).then_inc(h_done, 1)
                if what == "out":
                    dve.wait_ge(down_done, STEPS * (n + 1))
                    dve.wait_ge(xt_in, 16)
                    if n >= 2:
                        dve.wait_ge(y_out[n % 2], 16 * (n // 2))
                    dve.scalar_tensor_tensor(out=y[:, n % 2, :], in0=y_ps[n % 2][:], scalar=vec[:, V_BO:V_BO + 1],
                                             in1=xt[:, cols(n)], op0=ALU.add, op1=ALU.add).then_inc(y_done, 1)

        @block.tensor
        def _(pe):
            def product(dst, column, width, moving, first=True, last=True, lo_moving=None):
                h_, l_ = wh[:, column:column + width], wl[:, column:column + width]
                pe.matmul(dst, h_, moving, start=first, stop=False)
                pe.matmul(dst, l_, moving, start=False, stop=False)
                return pe.matmul(dst, h_, lo_moving, start=False, stop=last)

            for what, n in plan:
                if what == "turn":
                    if n == 0:
                        pe.wait_ge(const_in, 48)
                        pe.wait_ge(norm_done, 1)
                    else:
                        pe.wait_ge(norm_pool, n)
                    if n == 3:
                        pe.wait_ge(xl_done, 1)
                    for q in range(SUB):
                        last = pe.transpose(turn_ps[n][:, q * P:(q + 1) * P], xn[:, n * SUB + q, :], idf[:])
                    last.then_inc(turned, 1)
                if what == "logits":
                    pe.wait_ge(xl_done, n + 1)
                    pe.wait_ge(wl_done, 1)
                    r = slice(C_ROUTE, C_ROUTE + ROUTE)
                    for q in range(n * SUB, (n + 1) * SUB):
                        t = slice(q * P, (q + 1) * P)
                        pe.matmul(logits[:, q, :], xh[:, t], wh[:, r], start=True, stop=False)
                        pe.matmul(logits[:, q, :], xl[:, t], wh[:, r], start=False, stop=False)
                        last = pe.matmul(logits[:, q, :], xh[:, t], wl[:, r], start=False, stop=True)
                    last.then_inc(logits_done, 1)
                if what == "spread":
                    pe.wait_ge(consts_done, 2)
                    pe.wait_ge(routed_done, 1)
                    pe.wait_ge(xl_done, 2)
                    for m in range(2):
                        for q in range(BLOCKS // 2):
                            last = pe.transpose(spread_ps[m][:].bitcast(BF16)[0:KSEL, q * P:(q + 1) * P],
                                                routed16[:, m * BLOCKS // 2 + q, :, :].rearrange("p a r -> p (a r)"),
                                                idb[:])
                        last.then_inc(spread_done, 1)
                if what == "delta":
                    pe.wait_ge(routed_t_done, 2)
                    pe.matmul(pair_ps[n][:], sels[:, PAIRS, :], routed_t[:, cols(2 * n)], start=True, stop=False)
                    pe.matmul(pair_ps[n][:], sels[:, PAIRS + 1, :], routed_t[:, cols(2 * n + 1)], start=False,
                              stop=True).then_inc(delta_done, 1)
                if what == "bproj":
                    pe.wait_ge(da_done, n + 1)
                    pe.wait_ge(wl_done, piece_of(C_B) + 1)
                    for m in range(2):
                        c = cols(2 * n + m)
                        last = product(pair_ps[n][:], C_B + m * P, P, xh[:, c], first=m == 0, last=m == 1,
                                       lo_moving=xl[:, c])
                    last.then_inc(b_done, 1)
                if what == "up":
                    b, e = divmod(n, STEPS)
                    c = cols(b)
                    pe.wait_ge(xl_done, b + 1)
                    if n >= 2:
                        pe.wait_ge(v_done, n - 1)
                    if e < PAIRS:
                        pe.wait_ge(wl_done, piece_of(C_UP + 256 * e) + 1)
                        product(gate_ps[n % 2][:], C_UP + 256 * e, P, xh[:, c], lo_moving=xl[:, c])
                        last = product(up_ps[n % 2][:], C_UP + 256 * e + P, P, xh[:, c], lo_moving=xl[:, c])
                    else:
                        pe.wait_ge(wl_done, piece_of(C_SHARED) + 1)
                        last = product(gate_ps[n % 2][:], C_SHARED + (b % 2) * P, P, xh[:, c], lo_moving=xl[:, c])
                    last.then_inc(up_done, 1)
                if what == "cast" and n % STEPS < PAIRS:
                    b, e = divmod(n, STEPS)
                    i = pairs_before(n)
                    pe.wait_ge(routed_t_done, 2)
                    pe.wait_ge(xl_done, 3)
                    if i:
                        pe.wait_ge(h_done, i)
                    pe.matmul(cast_ps[:], sels[:, e, :], routed_t[:, cols(b)], start=True,
                              stop=True).then_inc(cast_done, 1)
                if what == "down":
                    b, e = divmod(n, STEPS)
                    pe.wait_ge(hl_done, n + 1)
                    if e == 0:
                        pe.wait_ge(wl_done, len(PIECES))
                        if b == 0:
                            pe.wait_ge(xl_done, 4)
                        if b == 1:
                            pe.wait_ge(bs_done, 1)
                        if b >= 2:
                            pe.wait_ge(y_done, b - 1)
                    column = C_DOWN + P * e if e < PAIRS else C_TAIL + P * (b % 2)
                    product(y_ps[b % 2][:], column, P, hh[:, n % SPLIT_BUFS, :], first=e == 0, last=e == PAIRS,
                            lo_moving=hl[:, n % SPLIT_BUFS, :]).then_inc(down_done, 1)


def layouts(a):
    zero = np.zeros((P, STATES), np.float32)
    x = a["L0_attn_x"].reshape(BATCH * SEQ, D)
    w13, w2 = a["L0_ffn_w13"], a["L0_ffn_w2"]
    gate_up = w13.reshape(PAIRS, 2, 2, INTER, D).transpose(4, 0, 2, 1, 3).reshape(D, PAIRS * 256)
    down = w2.reshape(PAIRS, 2, D, INTER).transpose(1, 3, 0, 2).reshape(P, PAIRS * D)
    gate_s, up_s = a["L0_ffn_w13_s"][:INTER].T, a["L0_ffn_w13_s"][INTER:].T
    wb, wo, w2_s, wd = a["L0_attn_WB"].T, a["L0_attn_Wo"].T, a["L0_ffn_w2_s"].T, a["L0_attn_Wd"].T
    weights = np.concatenate([
        a["L0_ffn_gate_w"].T, wd, wd, gate_up, gate_s, up_s, up_s, gate_s, wb, zero, zero, wb, down,
        np.concatenate([wo, w2_s]), np.concatenate([w2_s, wo])], axis=1)
    vectors = np.concatenate([
        np.tile(a["L0_attn_A_log"], 2)[:, None], np.tile(a["L0_attn_bB"], 2)[:, None], a["L0_attn_bo"][:, None],
        np.tile(a["L0_attn_bd"], P)[:, None], np.tile(a["L0_ffn_gate_b"][None, :], (P, 1))], axis=1)
    sel = np.zeros((KSEL, SELECTORS, P), np.float32)
    for part in range(PARTS):
        for e in range(EXPERTS):
            sel[part * ROW + e, e // 2, (e % 2) * INTER:(e % 2 + 1) * INTER] = 1
        sel[part * ROW + EXPERTS, PAIRS, 0:STATES] = 1
        sel[part * ROW + EXPERTS, PAIRS + 1, STATES:P] = 1
    return {
        "x_rows": x.reshape(BLOCKS, P, D).transpose(1, 0, 2),
        "x_cols": x.T,
        "weights": weights,
        "vectors": vectors,
        "sel": sel,
        "ident": np.eye(P, dtype=np.float32),
    }


def kernel(**inputs):
    import concourse.bacc as bacc
    from concourse.bass_utils import run_bass_kernel_spmd

    arrays = {k: np.ascontiguousarray(v) for k, v in layouts({k: np.asarray(v) for k, v in inputs.items()}).items()}
    nc = bacc.Bacc("TRN2", target_bir_lowering=False, num_devices=1)
    args = [nc.dram_tensor(k, v.shape, mybir.dt.from_np(v.dtype), kind="ExternalInput").ap()
            for k, v in arrays.items()]
    out = nc.dram_tensor("out", (D, BATCH * SEQ), F32, kind="ExternalOutput").ap()
    build(nc, *args, out)
    result = run_bass_kernel_spmd(nc, [arrays], core_ids=[0]).results[0]["out"]
    return np.ascontiguousarray(result.T).reshape(BATCH, SEQ, D)
```

```python
from contextlib import ExitStack

import numpy as np

import concourse.bass as bass
from concourse import mybir

F32 = mybir.dt.float32
F32R = mybir.dt.float32r
BF16 = mybir.dt.bfloat16
ALU = mybir.AluOpType
ACT = mybir.ActivationFunctionType
AX_X = mybir.AxisListType.X

P = 128
BATCH, SEQ, D = 4, 512, 128
STATES = 64
EXPERTS, INTER, TOPK = 16, 64, 4
ROUTE_SCALE = 2.5
ATTN_EPS, LN_EPS = 1e-6, 1e-5

TILE = SEQ
TILES = BATCH
SUB = TILE // P
BLOCKS = TILES * SUB
PAIRS = EXPERTS // 2
STEPS = PAIRS + 1
GROUPS = BATCH // 2
ROUTE = EXPERTS + 1
PARTS = 3
ROW = EXPERTS + 1
KSEL = PARTS * ROW
TAKEN = -3.0e38
FILLER = -2.0e38
WIDE = EXPERTS + 8 - TOPK

C_PROJ = 3 * 256
C_SHARED = (PAIRS + 1) * 256
C_DOWN = C_SHARED + 256
C_TAIL = C_DOWN + PAIRS * 128
C_END = C_TAIL + 256
LOADS = [(0, 512), (512, 1536), (1536, C_DOWN), (C_DOWN, C_END)]
PIECES = [(c, c + 256) for c in range(0, C_DOWN, 256)] + [(C_DOWN, C_DOWN + 512), (C_DOWN + 512, C_TAIL),
                                                          (C_TAIL, C_END)]


def up_column(e):
    return 256 * e if 256 * e < C_PROJ else 256 * (e + 1)


V_ALOG, V_BB, V_BO, V_BD, V_GB = 0, 1, 2, 3, 4
V_END = V_GB + EXPERTS
SELECTORS = PAIRS + 2

SILU_BUFS = 3
V_BUFS = 18
H_BUFS = 3
SPLIT_BUFS = 4
TAILS = [((2, 5), 0), ((1, 2), 1), ((3, 3), 2), ((3, 7), 3)]
LEAD = 2


def piece_of(column):
    return next(n for n, (a, b) in enumerate(PIECES) if a <= column < b)


def load_of(piece):
    return next(n for n, (a, b) in enumerate(LOADS) if a <= PIECES[piece][0] < b)


DOWNS = [(b, e) for b in range(TILES) for e in range(PAIRS)]
for after, b in TAILS:
    DOWNS.insert(DOWNS.index(after) + 1, (b, PAIRS))
LAST_OF = [max(p for p, (tile, _) in enumerate(DOWNS) if tile == b) for b in range(TILES)]
FIRST_OF = [min(p for p, (tile, _) in enumerate(DOWNS) if tile == b) for b in range(TILES)]

PE_ORDER = """
turn0 turn1 proj0 turn2 gate0 proj1 turn3 up0 gate1 proj2 up1 proj3 gate2 up2 gate3 logits0 gate4 up3 up4 gate5
up5 gate6 up6 gate7 gate8 up7 gate9 up9 gate10 gate11 up10 up11 spread0 gate12 spread1 cast0 delta0 gate13 cast1
delta1 up12 cast2 up13 down0 gate14 cast3 gate15 up14 cast4 up15 down1 gate16 cast5 gate17 cast6 up16 down2
cast7 down3 gate18 cast8 up18 gate19 down4 cast9 down5 gate20 cast10 down6 up19 cast12 up20 down7 gate21 down8
cast13 up21 down9 cast14 down10 gate22 cast15 down11 up22 down12 cast16 down13 gate23 down14 cast17 gate24 up23
cast18 up24 down15 gate25 cast19 down16 gate26 cast20 up25 down17 cast21 down18 gate27 down19 cast22 up27 gate28
cast24 up28 down20 cast25 down21 gate29 cast26 up29 gate30 cast27 down22 gate31 cast28 down23 up30 cast29 up31
down24 gate32 down25 cast31 up32 down26 cast32 down27 gate33 cast33 gate34 down28 up33 down29 up34 gate35 cast34
down30 down31 down32 down33 down34 down35"""
ACT_ORDER = """
split0 split1 split2 split3 split4 split5 turn0 split6 norm1 split7 norm2 turn1 norm3 turn2 proj0 turn3 proj1
up0 proj2 up1 proj3 up2 consts0 up3 split8 route0 up4 split9 up5 split10 split11 split12 up6 up7 up8 up9 up10
up11 spread0 up12 spread1 cast0 up13 decay0 cast1 up14 cast2 up15 cast3 cast4 up16 cast5 up17 cast6 cast7 up18
up19 cast8 cast9 up20 cast10 cast11 up21 cast12 cast13 cast14 up22 cast15 up23 cast16 up24 cast17 cast18 up25
cast19 up26 cast20 cast21 up27 cast22 up28 cast23 cast24 cast25 up29 up30 cast26 up31 cast27 cast28 up32 cast29
cast30 cast31 up33 up34 cast32 cast33 up35 cast34 cast35"""
DVE_ORDER = """
stats0 stats1 norm0 stats2 norm1 stats3 norm2 turn0 norm3 turn1 turn2 turn3 up0 up1 up2 route0 up3 route1 soft0
route2 up4 route3 up5 route4 up6 route5 soft1 route6 up7 route7 up8 route8 soft2 up9 route9 route10 up10 up11
cast0 cast1 up12 cast2 up13 cast3 attn0 attn1 up14 attn10 up15 cast4 attn5 attn4 cast5 attn3 cast6 up16 cast7
up17 attn2 cast8 up18 attn11 cast9 attn7 cast10 up19 attn8 cast12 attn12 cast13 up20 cast14 up21 attn15 cast15
attn13 up22 cast16 attn14 cast17 up23 cast18 up24 attn17 cast19 cast20 up25 up26 cast21 attn18 cast22 up27
cast24 up28 cast25 cast26 up29 cast27 cast28 out0 up30 out1 up31 cast29 cast31 up32 cast32 up33 cast33 up34
cast34 up35 out2 out3"""
POOL_ORDER = """
split0 stats0 split1 stats1 split2 split3 stats2 split4 stats3 split5 split6 split7 split8 split9 split10
split11 split12 cast0 cast1 attn1 cast2 cast3 cast4 cast5 cast6 cast7 attn6 cast8 attn7 cast9 attn11 cast10
cast11 cast12 cast13 cast14 cast15 attn16 cast16 cast17 cast18 attn17 cast19 cast20 cast21 cast22 cast23 cast24
cast25 cast26 cast27 cast28 cast29 cast30 cast31 cast32 cast33 cast34 cast35"""


def items(text):
    return [(x.rstrip("0123456789"), int(x[len(x.rstrip("0123456789")):])) for x in text.split()]


def build(nc, x_rows, x_cols, weights, vectors, sel, ident, out):
    with ExitStack() as ctx:
        def sb(name, shape, dt=F32):
            return ctx.enter_context(nc.sbuf_tensor(name, shape, dt))

        def sem(name):
            return ctx.enter_context(nc.semaphore(name))

        xr = sb("xr", [P, BLOCKS, D])
        xt = sb("xt", [P, BATCH * SEQ])
        w = sb("w", [P, C_END])
        wh = sb("wh", [P, C_END], F32R)
        wl = sb("wl", [P, C_END], F32R)
        vec = sb("vec", [P, V_END])
        sels = sb("sels", [KSEL, SELECTORS, P], BF16)
        idf = sb("idf", [P, P])
        idb = sb("idb", [P, P], BF16)
        stats = sb("stats", [P, BLOCKS, 6])
        moments = sb("moments", [P, BLOCKS, 2])
        var_eps = sb("var_eps", [P, BLOCKS])
        neg_mean = sb("neg_mean", [P, BLOCKS])
        minus_half = sb("minus_half", [P, SUB])
        rstd = sb("rstd", [P, BLOCKS])
        shift = sb("shift", [P, BLOCKS])
        xh = sb("xh", [P, BATCH * SEQ], F32R)
        xl = sb("xl", [P, BATCH * SEQ], F32R)
        zb = sb("zb", [P, BLOCKS + 1])
        zabs = sb("zabs", [P, BLOCKS + 1])
        zexp = sb("zexp", [P, BLOCKS + 1])
        zexp1 = sb("zexp1", [P, BLOCKS + 1])
        zexp1_rec = sb("zexp1_rec", [P, BLOCKS + 1])
        zlost = sb("zlost", [P, BLOCKS + 1])
        zfix = sb("zfix", [P, BLOCKS + 1])
        zln = sb("zln", [P, BLOCKS + 1])
        zlog1p = sb("zlog1p", [P, BLOCKS + 1])
        softplus = sb("softplus", [P, BLOCKS + 1])
        a_neg = sb("a_neg", [P, 1])
        a_eps = sb("a_eps", [P, 1])
        a_rec = sb("a_rec", [P, 1])
        logits_t = sb("logits_t", [ROUTE, BATCH * SEQ])
        lexp = sb("lexp", [P, BLOCKS, EXPERTS])
        lexp1 = sb("lexp1", [P, BLOCKS, EXPERTS])
        scores = sb("scores", [P, BLOCKS, EXPERTS])
        biased = sb("biased", [P, BLOCKS, WIDE])
        top8 = sb("top8", [P, BLOCKS, 8])
        marked = sb("marked", [P, BLOCKS, WIDE])
        chosen = sb("chosen", [P, BLOCKS, EXPERTS])
        picked = sb("picked", [P, BLOCKS, EXPERTS])
        total = sb("total", [P, BLOCKS])
        total_rec = sb("total_rec", [P, BLOCKS])
        routed = sb("routed", [P, BLOCKS, ROW])
        rest1 = sb("rest1", [P, BLOCKS, ROW])
        rest2 = sb("rest2", [P, BLOCKS, ROW])
        routed16 = sb("routed16", [P, BLOCKS, PARTS, ROW], BF16)
        routed_t = sb("routed_t", [KSEL, BATCH * SEQ], BF16)
        silu = sb("silu", [P, SILU_BUFS, TILE])
        v = sb("v", [P, V_BUFS, TILE])
        h = sb("h", [P, H_BUFS, TILE])
        hh = sb("hh", [P, SPLIT_BUFS, TILE], F32R)
        hl = sb("hl", [P, SPLIT_BUFS, TILE], F32R)
        tail = sb("tail", [P, TILES, TILE])
        sels_in = tail[0:KSEL, 0:3, :].rearrange("k t n -> k (t n)")[:, 0:SELECTORS * P].rearrange(
            "k (s n) -> k s n", s=SELECTORS)
        ones = sb("ones", [P, TILE])
        zeros = sb("zeros", [P, TILE])
        da = sb("da", [P, GROUPS, TILE])
        ct = sb("ct", [P, GROUPS, TILE + 1])
        ct_eps = sb("ct_eps", [P, GROUPS, TILE])
        ct_rec = sb("ct_rec", [P, GROUPS, TILE])
        bs = sb("bs", [P, GROUPS, TILE])
        db = sb("db", [P, GROUPS, TILE])
        z, s, state = ct_eps, da, bs

        def bank(name):
            return ctx.enter_context(nc.psum_tensor(name, [P, TILE], F32))

        gate_ps = [bank("gate0"), bank("gate1")]
        up_ps = [bank("up0"), bank("up1")]
        cast_ps = bank("cast")
        y0, y1, misc_ps = bank("y0"), bank("y1"), bank("misc")
        y_ps = [y0, y1, misc_ps, y0]
        turn_ps = [y0, y1, y0, y1]
        proj_ps = [misc_ps, cast_ps, misc_ps, cast_ps]
        logits = y0[:, 0:BLOCKS * ROUTE].rearrange("p (q r) -> p q r", r=ROUTE)
        spread_ps = [y1, misc_ps]
        pair_ps = [y1, misc_ps]

        consts_done = sem("consts_done")
        x_in = [sem(f"x_in{b}") for b in range(TILES)]
        w_in = [sem(f"w_in{n}") for n in range(len(LOADS))]
        const_in = sem("const_in")
        ident_in = sem("ident_in")
        xt_in = sem("xt_in")
        filled = sem("filled")
        var_done = sem("var_done")
        rstd_done = sem("rstd_done")
        norm_done = sem("norm_done")
        shift_done = sem("shift_done")
        norm_act = sem("norm_act")
        turned = sem("turned")
        xh_done = sem("xh_done")
        xl_done = sem("xl_done")
        wh_done = sem("wh_done")
        wl_done = sem("wl_done")
        logits_done = sem("logits_done")
        zb_done = sem("zb_done")
        exp_done = sem("exp_done")
        act_step = sem("act_step")
        dve_step = sem("dve_step")
        pool_step = sem("pool_step")
        routed_done = sem("routed_done")
        a_done = sem("a_done")
        spread_done = sem("spread_done")
        routed_t_done = sem("routed_t_done")
        delta_done = sem("delta_done")
        da_done = sem("da_done")
        proj_done = sem("proj_done")
        bs_done = sem("bs_done")
        logits_t_done = sem("logits_t_done")
        ct_done = sem("ct_done")
        ct_eps_done = sem("ct_eps_done")
        db_done = sem("db_done")
        rec_done = sem("rec_done")
        z_done = sem("z_done")
        s_done = sem("s_done")
        state_done = sem("state_done")
        attn_done = sem("attn_done")
        gate_done = sem("gate_done")
        up_done = sem("up_done")
        silu_done = sem("silu_done")
        v_done = sem("v_done")
        cast_done = sem("cast_done")
        h_done = sem("h_done")
        hh_done = sem("hh_done")
        hl_done = sem("hl_done")
        down_done = sem("down_done")
        y_done = sem("y_done")
        y_out = [sem(f"y_out{b}") for b in range(TILES)]

        block = ctx.enter_context(nc.Block())

        def position(i):
            return DOWNS.index(divmod(i, PAIRS))

        def cols(b):
            return slice(b * TILE, (b + 1) * TILE)

        def shared_half(b):
            return slice(64, 128) if b % 2 == 0 else slice(0, 64)

        def attn_half(b):
            return slice(0, 64) if b % 2 == 0 else slice(64, 128)

        @block.sync
        def _(sp):
            def load_x(b):
                sp.dma_start(xr[:, b * SUB:(b + 1) * SUB, :], x_rows[:, b * SUB:(b + 1) * SUB, :]).then_inc(x_in[b], 16)

            def load_w(n):
                a, b = LOADS[n]
                sp.dma_start(w[:, a:b], weights[:, a:b]).then_inc(w_in[n], 16)

            load_x(0)
            load_w(0)
            load_x(1)
            sp.dma_start(idf[:], ident).then_inc(ident_in, 16)
            load_x(2)
            load_w(1)
            load_x(3)
            load_w(2)
            sp.dma_start(vec[:], vectors).then_inc(const_in, 16)
            sp.dma_start(sels_in, sel).then_inc(const_in, 16)
            load_w(3)
            sp.dma_start(xt[:], x_cols).then_inc(xt_in, 16)
            for b in range(TILES):
                sp.wait_ge(y_done, b + 1)
                sp.dma_start(out[:, cols(b)], xt[:, cols(b)]).then_inc(y_out[b], 16)
            for b in range(TILES):
                sp.wait_ge(y_out[b], 16)

        @block.gpsimd
        def _(pool):
            steps = [0]

            def link(ins):
                steps[0] += 1
                ins.then_inc(pool_step, 1)
                pool.wait_ge(pool_step, steps[0])

            pool.memset(minus_half[:], -0.5).then_inc(filled, 1)
            pool.memset(ones[:], 1.0).then_inc(filled, 1)
            pool.memset(zeros[:], 0.0).then_inc(filled, 1)
            pool.memset(ct[:, :, 0:1], 1.0).then_inc(filled, 1)
            pool.memset(biased[:, :, EXPERTS:WIDE], FILLER).then_inc(filled, 1)
            pool.wait_ge(filled, 5)
            for what, n in items(POOL_ORDER):
                if what == "stats":
                    q = slice(n * SUB, (n + 1) * SUB)
                    pool.wait_ge(var_done, n + 1)
                    pool.tensor_tensor(rstd[:, q], var_eps[:, q], minus_half[:], ALU.pow).then_inc(rstd_done, 1)
                if what == "split":
                    a, b = PIECES[n]
                    pool.wait_ge(wh_done, n + 1)
                    pool.tensor_tensor(wl[:, a:b], w[:, a:b], wh[:, a:b].bitcast(F32),
                                       ALU.subtract).then_inc(wl_done, 1)
                if what == "attn" and n % 10 == 1:
                    g = n // 10
                    pool.wait_ge(ct_done, g + 1)
                    pool.tensor_scalar(ct_eps[:, g, :], ct[:, g, 0:TILE], ATTN_EPS, 1.0, ALU.add,
                                       ALU.mult).then_inc(ct_eps_done, 1)
                if what == "attn" and n % 10 == 6:
                    g = n // 10
                    pool.wait_ge(rec_done, 4 * (g + 1))
                    pool.wait_ge(db_done, g + 1)
                    pool.tensor_tensor(z[:, g, :], db[:, g, :], ct_rec[:, g, :], ALU.mult).then_inc(z_done, 1)
                if what == "attn" and n % 10 == 7:
                    g = n // 10
                    pool.wait_ge(s_done, g + 1)
                    pool.tensor_tensor(state[:, g, :], ct[:, g, 0:TILE], s[:, g, :],
                                       ALU.mult).then_inc(state_done, 1)
                if what == "cast":
                    b, e = DOWNS[n]
                    pool.wait_ge(hh_done, n + 1)
                    if n >= SPLIT_BUFS:
                        pool.wait_ge(down_done, n - SPLIT_BUFS + 1)
                    src = h[:, (b * PAIRS + e) % H_BUFS, :] if e < PAIRS else tail[:, b, :]
                    pool.tensor_tensor(hl[:, n % SPLIT_BUFS, :], src, hh[:, n % SPLIT_BUFS, :].bitcast(F32),
                                       ALU.subtract).then_inc(hl_done, 1)

        @block.scalar
        def _(act):
            steps = [0]

            def link(ins):
                steps[0] += 1
                ins.then_inc(act_step, 1)
                act.wait_ge(act_step, steps[0])

            act.preload_act_table_set("silu_and_others")
            for what, n in items(ACT_ORDER):
                if what == "norm" and n > 0:
                    act.wait_ge(shift_done, n)
                    for q in range(n * SUB, (n + 1) * SUB):
                        last = act.activation(xr[:, q, :], xr[:, q, :], ACT.Identity, bias=shift[:, q:q + 1],
                                              scale=rstd[:, q:q + 1])
                    last.then_inc(norm_act, 1)
                if what == "split":
                    a, b = PIECES[n]
                    act.wait_ge(w_in[load_of(n)], 16)
                    act.activation(wh[:, a:b], w[:, a:b], ACT.Copy).then_inc(wh_done, 1)
                if what == "consts":
                    act.wait_ge(const_in, 32)
                    act.wait_ge(ident_in, 16)
                    act.activation(sels[:], sels_in, ACT.Copy).then_inc(consts_done, 1)
                    act.activation(idb[:], idf[:], ACT.Copy).then_inc(consts_done, 1)
                if what == "turn":
                    act.wait_ge(turned, n + 1)
                    act.activation(xh[:, cols(n)], turn_ps[n][:], ACT.Copy).then_inc(xh_done, 1)
                if what == "route" and n == 0:
                    act.preload_act_table_set("natural_log_exp_and_others")
                    act.wait_ge(zb_done, 1)
                    act.activation(lexp[:], logits[:, :, 0:EXPERTS], ACT.Exp, scale=-1.0).then_inc(exp_done, 1)
                    link(act.activation(zabs[:], zb[:], ACT.Abs))
                    link(act.activation(zexp[:], zabs[:], ACT.Exp, scale=-1.0))
                    act.activation(zln[:], zexp[:], ACT.Ln, bias=1.0).then_inc(exp_done, 1)
                    act.preload_act_table_set("silu_and_others")
                if what == "spread":
                    act.wait_ge(spread_done, n + 1)
                    act.activation(routed_t[:, 2 * n * TILE:(2 * n + 2) * TILE],
                                   spread_ps[n][:].bitcast(BF16)[0:KSEL, :], ACT.Copy).then_inc(routed_t_done, 1)
                if what == "decay":
                    act.preload_act_table_set("natural_log_exp_and_others")
                    act.wait_ge(a_done, 1)
                    for g in range(GROUPS):
                        act.wait_ge(delta_done, g + 1)
                        act.activation(da[:, g, :], pair_ps[g][:], ACT.Exp, scale=a_neg[:, 0:1]).then_inc(da_done, 1)
                    act.preload_act_table_set("silu_and_others")
                if what == "proj":
                    act.wait_ge(proj_done, n + 1)
                    half, other = attn_half(n), shared_half(n)
                    act.activation(logits_t[:, cols(n)], proj_ps[n][other.start:other.start + ROUTE, :], ACT.Copy).then_inc(
                        logits_t_done, 1)
                    if n == 0:
                        act.wait_ge(const_in, 32)
                    act.activation(bs[half, n // 2, :], proj_ps[n][half, :], ACT.Identity,
                                   bias=vec[half, V_BB:V_BB + 1]).then_inc(bs_done, 1)
                if what == "up":
                    b, e = divmod(n, STEPS)
                    act.wait_ge(gate_done, n + 1)
                    if n >= SILU_BUFS:
                        act.wait_ge(v_done, n - SILU_BUFS + 1)
                    if e < PAIRS:
                        act.activation(silu[:, n % SILU_BUFS, :], gate_ps[n % 2][:], ACT.Silu).then_inc(silu_done, 1)
                    else:
                        act.activation(silu[shared_half(b), n % SILU_BUFS, :], gate_ps[n % 2][attn_half(b), :],
                                       ACT.Silu).then_inc(silu_done, 1)
                if what == "cast":
                    b, e = DOWNS[n]
                    if e < PAIRS:
                        act.wait_ge(h_done, b * PAIRS + e + 1)
                    else:
                        act.wait_ge(v_done, b * STEPS + STEPS)
                        act.wait_ge(attn_done, b + 1)
                    if n >= SPLIT_BUFS:
                        act.wait_ge(down_done, n - SPLIT_BUFS + 1)
                    src = h[:, (b * PAIRS + e) % H_BUFS, :] if e < PAIRS else tail[:, b, :]
                    act.activation(hh[:, n % SPLIT_BUFS, :], src, ACT.Copy).then_inc(hh_done, 1)

        @block.vector
        def _(dve):
            steps = [0]

            def link(ins):
                steps[0] += 1
                ins.then_inc(dve_step, 1)
                dve.wait_ge(dve_step, steps[0])

            for what, n in items(DVE_ORDER):
                if what == "stats":
                    dve.wait_ge(x_in[n], 16)
                    qs = range(n * SUB, (n + 1) * SUB)
                    for q in qs:
                        last = dve.bn_stats(stats[:, q, :], xr[:, q, :])
                    link(last)
                    for q in qs:
                        last = dve.bn_aggr(moments[:, q, :], stats[:, q, :])
                    link(last)
                    dve.tensor_scalar(neg_mean[:, qs.start:qs.stop], moments[:, qs.start:qs.stop, 0], -1.0, None,
                                      ALU.mult)
                    dve.tensor_scalar(var_eps[:, qs.start:qs.stop], moments[:, qs.start:qs.stop, 1], LN_EPS, None,
                                      ALU.add).then_inc(var_done, 1)
                if what == "norm" and n == 0:
                    dve.wait_ge(rstd_done, 1)
                    dve.wait_ge(var_done, 1)
                    for q in range(SUB):
                        last = dve.tensor_scalar(xr[:, q, :], xr[:, q, :], neg_mean[:, q:q + 1],
                                                 rstd[:, q:q + 1], ALU.add, ALU.mult)
                    last.then_inc(norm_done, 1)
                if what == "norm" and n > 0:
                    q = slice(n * SUB, (n + 1) * SUB)
                    dve.wait_ge(rstd_done, n + 1)
                    dve.tensor_tensor(shift[:, q], neg_mean[:, q], rstd[:, q], ALU.mult).then_inc(shift_done, 1)
                if what == "turn":
                    dve.wait_ge(xh_done, n + 1)
                    dve.tensor_tensor(xl[:, cols(n)], turn_ps[n][:], xh[:, cols(n)].bitcast(F32),
                                      ALU.subtract).then_inc(xl_done, 1)
                if what == "route" and n == 0:
                    dve.wait_ge(const_in, 32)
                    dve.wait_ge(logits_done, 1)
                    dve.wait_ge(filled, 5)
                    dve.tensor_copy(zb[:, BLOCKS:BLOCKS + 1], vec[:, V_ALOG:V_ALOG + 1])
                    dve.tensor_scalar(zb[:, 0:BLOCKS], logits[:, :, EXPERTS], vec[:, V_BD:V_BD + 1], None,
                                      ALU.add).then_inc(zb_done, 1)
                if what == "route" and n == 1:
                    dve.wait_ge(exp_done, 1)
                    link(dve.tensor_scalar(lexp1[:], lexp[:], 1.0, None, ALU.add))
                if what == "route" and n in (1, 2):
                    q = slice((n - 1) * BLOCKS // 2, n * BLOCKS // 2)
                    link(dve.reciprocal(scores[:, q, :], lexp1[:, q, :]))
                if what == "route" and n == 3:
                    link(dve.tensor_tensor(biased[:, :, 0:EXPERTS], scores[:],
                                           vec[:, None, V_GB:V_END].to_broadcast([P, BLOCKS, EXPERTS]), ALU.add))
                if what == "route" and n in (3, 4):
                    for q in range((n - 3) * BLOCKS // 2, (n - 2) * BLOCKS // 2):
                        last = dve.max(top8[:, q, :], biased[:, q, 0:EXPERTS])
                    link(last)
                if what == "route" and n == 4:
                    link(dve.memset(top8[:, :, TOPK:8], FILLER))
                if what == "route" and n in (5, 6):
                    for q in range((n - 5) * BLOCKS // 2, (n - 4) * BLOCKS // 2):
                        last = dve.match_replace(marked[:, q, :], top8[:, q, :], biased[:, q, :], TAKEN)
                    link(last)
                if what == "route" and n == 7:
                    link(dve.tensor_tensor(chosen[:], marked[:, :, 0:EXPERTS], biased[:, :, 0:EXPERTS],
                                           ALU.not_equal))
                    link(dve.tensor_tensor(picked[:], scores[:], chosen[:], ALU.mult))
                if what == "route" and n == 8:
                    link(dve.tensor_reduce(total[:], picked[:], AX_X, ALU.add))
                    link(dve.reciprocal(total_rec[:], total[:]))
                    link(dve.scalar_tensor_tensor(out=routed[:, :, 0:EXPERTS], in0=picked[:], scalar=ROUTE_SCALE,
                                                  in1=total_rec[:, :, None].to_broadcast([P, BLOCKS, EXPERTS]),
                                                  op0=ALU.mult, op1=ALU.mult))
                if what == "soft" and n == 0:
                    dve.wait_ge(exp_done, 2)
                    link(dve.tensor_scalar(zexp1[:], zexp[:], 1.0, None, ALU.add))
                    link(dve.scalar_tensor_tensor(out=zlost[:], in0=zexp1[:], scalar=1.0, in1=zexp[:],
                                                  op0=ALU.subtract, op1=ALU.subtract))
                    link(dve.reciprocal(zexp1_rec[:], zexp1[:]))
                    link(dve.tensor_tensor(zfix[:], zlost[:], zexp1_rec[:], ALU.mult))
                if what == "soft" and n == 1:
                    link(dve.tensor_tensor(zlog1p[:], zln[:], zfix[:], ALU.subtract))
                    link(dve.scalar_tensor_tensor(out=softplus[:], in0=zb[:], scalar=0.0, in1=zlog1p[:], op0=ALU.max,
                                                  op1=ALU.add))
                    link(dve.tensor_copy(routed[:, :, EXPERTS], softplus[:, 0:BLOCKS]))
                if what == "soft" and n == 2:
                    link(dve.tensor_scalar(a_neg[:], softplus[:, BLOCKS:BLOCKS + 1], -1.0, None, ALU.mult))
                    link(dve.tensor_scalar(a_eps[:], a_neg[:], ATTN_EPS, None, ALU.add))
                    dve.reciprocal(a_rec[:], a_eps[:]).then_inc(a_done, 1)
                if what == "route" and n == 9:
                    link(dve.tensor_copy(routed16[:, :, 0, :], routed[:]))
                    link(dve.tensor_tensor(rest1[:], routed[:], routed16[:, :, 0, :], ALU.subtract))
                    link(dve.tensor_copy(routed16[:, :, 1, :], rest1[:]))
                if what == "route" and n == 10:
                    link(dve.tensor_tensor(rest2[:], rest1[:], routed16[:, :, 1, :], ALU.subtract))
                    dve.tensor_copy(routed16[:, :, 2, :], rest2[:]).then_inc(routed_done, 1)
                if what == "attn":
                    g, part = divmod(n, 10)
                    if part == 0:
                        dve.wait_ge(da_done, g + 1)
                        dve.tensor_tensor_scan(ct[:, g, 1:TILE + 1], da[:, g, :], zeros[:], 1.0, ALU.mult,
                                               ALU.add).then_inc(ct_done, 1)
                    if part == 1:
                        dve.wait_ge(bs_done, 2 * (g + 1))
                        dve.scalar_tensor_tensor(out=db[:, g, :], in0=da[:, g, :], scalar=1.0, in1=bs[:, g, :],
                                                 op0=ALU.subtract, op1=ALU.mult).then_inc(db_done, 1)
                    if 2 <= part < 6:
                        c = slice((part - 2) * P, (part - 1) * P)
                        dve.wait_ge(ct_eps_done, g + 1)
                        dve.reciprocal(ct_rec[:, g, c], ct_eps[:, g, c]).then_inc(rec_done, 1)
                    if part == 7:
                        dve.wait_ge(z_done, g + 1)
                        dve.tensor_tensor_scan(s[:, g, :], ones[:], z[:, g, :], 0.0, ALU.mult,
                                               ALU.add).then_inc(s_done, 1)
                    if part == 8:
                        dve.wait_ge(state_done, g + 1)
                        dve.wait_ge(a_done, 1)
                        for b in (2 * g, 2 * g + 1):
                            half = attn_half(b)
                            dve.wait_ge(consts_done, 1)
                            dve.scalar_tensor_tensor(out=tail[half, b, :], in0=ct[half, g, 0:TILE],
                                                     scalar=a_rec[half, 0:1], in1=state[half, g, :], op0=ALU.mult,
                                                     op1=ALU.mult).then_inc(attn_done, 1)
                if what == "up":
                    b, e = divmod(n, STEPS)
                    dve.wait_ge(silu_done, n + 1)
                    if e < PAIRS:
                        dve.wait_ge(up_done, b * PAIRS + e + 1)
                        dve.tensor_tensor(v[:, (b * PAIRS + e) % V_BUFS, :], silu[:, n % SILU_BUFS, :],
                                          up_ps[n % 2][:], ALU.mult).then_inc(v_done, 1)
                    else:
                        half = shared_half(b)
                        dve.wait_ge(consts_done, 1)
                        dve.tensor_tensor(tail[half, b, :], silu[half, n % SILU_BUFS, :], gate_ps[n % 2][half, :],
                                          ALU.mult).then_inc(v_done, 1)
                if what == "cast" and DOWNS[n][1] < PAIRS:
                    b, e = DOWNS[n]
                    i = b * PAIRS + e
                    dve.wait_ge(cast_done, i + 1)
                    dve.wait_ge(v_done, b * STEPS + e + 1)
                    if i >= H_BUFS:
                        dve.wait_ge(hl_done, position(i - H_BUFS) + 1)
                    dve.tensor_tensor(h[:, i % H_BUFS, :], v[:, i % V_BUFS, :], cast_ps[:],
                                      ALU.mult).then_inc(h_done, 1)
                if what == "out":
                    dve.wait_ge(down_done, LAST_OF[n] + 1)
                    dve.wait_ge(xt_in, 16)
                    dve.scalar_tensor_tensor(out=xt[:, cols(n)], in0=y_ps[n][:], scalar=vec[:, V_BO:V_BO + 1],
                                             in1=xt[:, cols(n)], op0=ALU.add, op1=ALU.add).then_inc(y_done, 1)

        @block.tensor
        def _(pe):
            def product(dst, column, width, moving, first=True, last=True, lo_moving=None):
                h_, l_ = wh[:, column:column + width], wl[:, column:column + width]
                pe.matmul(dst, h_, moving, start=first, stop=False)
                pe.matmul(dst, l_, moving, start=False, stop=False)
                return pe.matmul(dst, h_, lo_moving, start=False, stop=last)

            for what, n in items(PE_ORDER):
                if what == "turn":
                    if n == 0:
                        pe.wait_ge(ident_in, 16)
                        pe.wait_ge(norm_done, 1)
                    else:
                        pe.wait_ge(norm_act, n)
                    if n >= 2:
                        pe.wait_ge(xl_done, n - 1)
                    for q in range(SUB):
                        last = pe.transpose(turn_ps[n][:, q * P:(q + 1) * P], xr[:, n * SUB + q, :], idf[:])
                    last.then_inc(turned, 1)
                if what == "proj":
                    pe.wait_ge(xl_done, n + 1)
                    pe.wait_ge(wl_done, piece_of(C_PROJ) + 1)
                    if n >= 2:
                        pe.wait_ge(bs_done, n - 1)
                    product(proj_ps[n][:], C_PROJ + P * (n % 2), P, xh[:, cols(n)],
                            lo_moving=xl[:, cols(n)]).then_inc(proj_done, 1)
                if what == "logits":
                    pe.wait_ge(xl_done, 3)
                    for b in range(TILES):
                        pe.wait_ge(logits_t_done, b + 1)
                        for q in range(b * SUB, (b + 1) * SUB):
                            last = pe.transpose(logits[:, q, :], logits_t[:, q * P:(q + 1) * P],
                                                idf[0:ROUTE, 0:ROUTE])
                    last.then_inc(logits_done, 1)
                if what == "spread":
                    if n == 0:
                        pe.wait_ge(consts_done, 2)
                        pe.wait_ge(routed_done, 1)
                    pe.wait_ge(*((xl_done, 4) if n == 0 else (bs_done, 3)))
                    for q in range(BLOCKS // 2):
                        last = pe.transpose(spread_ps[n][:].bitcast(BF16)[0:KSEL, q * P:(q + 1) * P],
                                            routed16[:, n * BLOCKS // 2 + q, :, :].rearrange("p a r -> p (a r)"),
                                            idb[:])
                    last.then_inc(spread_done, 1)
                if what == "delta":
                    pe.wait_ge(routed_t_done, n + 1)
                    pe.matmul(pair_ps[n][:], sels[:, PAIRS, :], routed_t[:, cols(2 * n)], start=True, stop=False)
                    pe.matmul(pair_ps[n][:], sels[:, PAIRS + 1, :], routed_t[:, cols(2 * n + 1)], start=False,
                              stop=True).then_inc(delta_done, 1)
                if what == "gate":
                    b, e = divmod(n, STEPS)
                    column = up_column(e) if e < PAIRS else C_SHARED + (b % 2) * P
                    pe.wait_ge(xl_done, b + 1)
                    pe.wait_ge(wl_done, piece_of(column) + 1)
                    if n >= 2:
                        pe.wait_ge(v_done, n - 1)
                    product(gate_ps[n % 2][:], column, P, xh[:, cols(b)], lo_moving=xl[:, cols(b)]).then_inc(
                        gate_done, 1)
                if what == "up":
                    b, e = divmod(n, STEPS)
                    if n >= 2:
                        pe.wait_ge(v_done, n - 1)
                    product(up_ps[n % 2][:], up_column(e) + P, P, xh[:, cols(b)], lo_moving=xl[:, cols(b)]).then_inc(
                        up_done, 1)
                if what == "cast" and DOWNS[n][1] < PAIRS:
                    b, e = DOWNS[n]
                    i = b * PAIRS + e
                    pe.wait_ge(routed_t_done, b // 2 + 1)
                    pe.wait_ge(bs_done, 4)
                    if i:
                        pe.wait_ge(h_done, i)
                    pe.matmul(cast_ps[:], sels[:, e, :], routed_t[:, cols(b)], start=True,
                              stop=True).then_inc(cast_done, 1)
                if what == "down":
                    b, e = DOWNS[n]
                    pe.wait_ge(hl_done, n + 1)
                    if e == 0:
                        if b == 0:
                            pe.wait_ge(wl_done, len(PIECES))
                            pe.wait_ge(exp_done, 1)
                        if b == 1:
                            pe.wait_ge(da_done, 1)
                        if b == 2:
                            pe.wait_ge(da_done, 2)
                        if b == 3:
                            pe.wait_ge(y_done, 1)
                    column = C_DOWN + P * e if e < PAIRS else C_TAIL + P * (b % 2)
                    product(y_ps[b][:], column, P, hh[:, n % SPLIT_BUFS, :], first=n == FIRST_OF[b], last=n == LAST_OF[b],
                            lo_moving=hl[:, n % SPLIT_BUFS, :]).then_inc(down_done, 1)


def layouts(a):
    x = a["L0_attn_x"].reshape(BATCH * SEQ, D)
    w13, w2 = a["L0_ffn_w13"], a["L0_ffn_w2"]
    gate_up = w13.reshape(PAIRS, 2, 2, INTER, D).transpose(4, 0, 2, 1, 3).reshape(D, PAIRS * 256)
    down = w2.reshape(PAIRS, 2, D, INTER).transpose(1, 3, 0, 2).reshape(P, PAIRS * D)
    gate_s, up_s = a["L0_ffn_w13_s"][:INTER].T, a["L0_ffn_w13_s"][INTER:].T
    wb, wo, w2_s, wd = a["L0_attn_WB"].T, a["L0_attn_Wo"].T, a["L0_ffn_w2_s"].T, a["L0_attn_Wd"].T
    route = np.concatenate([a["L0_ffn_gate_w"].T, wd, np.zeros((D, STATES - ROUTE), np.float32)], axis=1)
    weights = np.concatenate([
        gate_up[:, :C_PROJ], wb, route, route, wb, gate_up[:, C_PROJ:], gate_s, up_s, up_s, gate_s, down,
        np.concatenate([wo, w2_s]), np.concatenate([w2_s, wo])], axis=1)
    vectors = np.concatenate([
        np.tile(a["L0_attn_A_log"], 2)[:, None], np.tile(a["L0_attn_bB"], 2)[:, None], a["L0_attn_bo"][:, None],
        np.tile(a["L0_attn_bd"], P)[:, None], np.tile(a["L0_ffn_gate_b"][None, :], (P, 1))], axis=1)
    sel = np.zeros((KSEL, SELECTORS, P), np.float32)
    for part in range(PARTS):
        for e in range(EXPERTS):
            sel[part * ROW + e, e // 2, (e % 2) * INTER:(e % 2 + 1) * INTER] = 1
        sel[part * ROW + EXPERTS, PAIRS, 0:STATES] = 1
        sel[part * ROW + EXPERTS, PAIRS + 1, STATES:P] = 1
    return {
        "x_rows": x.reshape(BLOCKS, P, D).transpose(1, 0, 2),
        "x_cols": x.T,
        "weights": weights,
        "vectors": vectors,
        "sel": sel,
        "ident": np.eye(P, dtype=np.float32),
    }


def kernel(**inputs):
    import concourse.bacc as bacc
    from concourse.bass_utils import run_bass_kernel_spmd

    arrays = {k: np.ascontiguousarray(v) for k, v in layouts({k: np.asarray(v) for k, v in inputs.items()}).items()}
    nc = bacc.Bacc("TRN2", target_bir_lowering=False, num_devices=1)
    args = [nc.dram_tensor(k, v.shape, mybir.dt.from_np(v.dtype), kind="ExternalInput").ap()
            for k, v in arrays.items()]
    out = nc.dram_tensor("out", (D, BATCH * SEQ), F32, kind="ExternalOutput").ap()
    build(nc, *args, out)
    result = run_bass_kernel_spmd(nc, [arrays], core_ids=[0]).results[0]["out"]
    return np.ascontiguousarray(result.T).reshape(BATCH, SEQ, D)
```

```python
from contextlib import ExitStack

import numpy as np

import concourse.bass as bass
from concourse import mybir

F32 = mybir.dt.float32
F32R = mybir.dt.float32r
BF16 = mybir.dt.bfloat16
ALU = mybir.AluOpType
ACT = mybir.ActivationFunctionType
AX_X = mybir.AxisListType.X

P = 128
BATCH, SEQ, D = 4, 512, 128
STATES = 64
EXPERTS, INTER, TOPK = 16, 64, 4
ROUTE_SCALE = 2.5
ATTN_EPS, LN_EPS = 1e-6, 1e-5

TILE = SEQ
TILES = BATCH
SUB = TILE // P
BLOCKS = TILES * SUB
PAIRS = EXPERTS // 2
STEPS = PAIRS + 1
GROUPS = BATCH // 2
ROUTE = EXPERTS + 1
PARTS = 3
ROW = EXPERTS + 1
KSEL = PARTS * ROW
TAKEN = -3.0e38
FILLER = -2.0e38
WIDE = EXPERTS + 8 - TOPK

C_PROJ = 3 * 256
C_SHARED = (PAIRS + 1) * 256
C_DOWN = C_SHARED + 256
C_TAIL = C_DOWN + PAIRS * 128
C_END = C_TAIL + 256
LOADS = [(0, 512), (512, 1536), (1536, C_DOWN), (C_DOWN, C_END)]
PIECES = [(c, c + 256) for c in range(0, C_DOWN, 256)] + [(C_DOWN, C_DOWN + 512), (C_DOWN + 512, C_TAIL),
                                                          (C_TAIL, C_END)]


def up_column(e):
    return 256 * e if 256 * e < C_PROJ else 256 * (e + 1)


V_ALOG, V_BB, V_BO, V_BD, V_GB = 0, 1, 2, 3, 4
V_END = V_GB + EXPERTS
SELECTORS = PAIRS + 2

CHUNKS = [(0, SUB // 2), (SUB // 2, SUB)] + [(b * SUB, (b + 1) * SUB) for b in range(1, TILES)]

OUTS = [(b * TILE, (b + 1) * TILE) for b in range(TILES - 1)] + [
    ((TILES - 1) * TILE, TILES * TILE - TILE // 2), (TILES * TILE - TILE // 2, TILES * TILE)]

HALF = BLOCKS // 2
ROUTE_STEPS = 16
SILU_BUFS = 3
V_BUFS = 18
H_BUFS = 3
SPLIT_BUFS = 4
WARM = (12, 5)
TAILS = [((2, 5), 0), ((2, 4), 1), ((3, 2), 2), ((3, 6), 3)]


def piece_of(column):
    return next(n for n, (a, b) in enumerate(PIECES) if a <= column < b)


def load_of(piece):
    return next(n for n, (a, b) in enumerate(LOADS) if a <= PIECES[piece][0] < b)


DOWNS = [(b, e) for b in range(TILES) for e in range(PAIRS)]
for after, b in TAILS:
    DOWNS.insert(DOWNS.index(after) + 1, (b, PAIRS))
LAST_OF = [max(p for p, (tile, _) in enumerate(DOWNS) if tile == b) for b in range(TILES)]
FIRST_OF = [min(p for p, (tile, _) in enumerate(DOWNS) if tile == b) for b in range(TILES)]

PE_ORDER = """
warm0 turn0 warm1 gate0 up0 proj0 gate1 up1 gate2 up2 turn1 gate3 up3 turn2 proj1 turn3 gate4 proj2 up4 proj3
gate5 gate6 up5 logits0 up6 gate7 up7 gate8 gate9 up9 gate10 up10 gate11 up11 gate12 up12 gate13 up13 gate14
up14 gate15 gate16 up15 up16 gate17 spread0 gate18 up18 cast0 delta0 gate19 cast1 up19 gate20 cast2 up20 gate21
cast3 spread1 up21 cast4 down0 down1 cast5 down2 delta1 cast6 down3 down4 cast7 gate22 gate23 cast8 down5 down6
cast9 up22 down7 cast10 up23 down8 cast11 gate24 down9 cast12 up24 down10 cast13 gate25 up25 cast14 down11
gate26 cast15 down12 down13 cast16 gate27 down14 cast17 up27 down15 cast18 gate28 up28 cast19 down16 gate29
cast20 down17 up29 cast22 down18 down19 cast24 gate30 down20 cast25 down21 gate31 cast26 down22 up30 cast27
down23 down24 up31 cast28 gate32 down25 cast30 up32 gate33 down26 cast31 down27 up33 cast32 gate34 up34 gate35
cast33 down28 down29 cast35 down30 down31 down32 down33 down34 down35"""
ACT_ORDER = """
table0 acalc0 table1 wh0 wh1 xh0 wh3 wh5 wh2 wh4 silu0 wh6 wh9 wh8 consts0 silu1 bs0 xh1 wh10 silu2 silu3 xh2
bs1 xh3 silu4 wh7 bs2 bs3 silu5 silu6 table2 sig0 table3 silu7 silu8 silu9 wh12 wh11 silu10 silu11 silu12 silu13
silu14 route11 silu15 route13 silu16 silu17 routedt0 silu18 route27 high0 silu19 route29 high1 silu20 high2
silu21 routedt1 high3 table4 decay0 high5 decay1 high6 table5 high7 silu22 square0 high8 silu23 high9 square1
high10 silu24 high12 silu25 silu26 high15 silu27 high16 high17 high18 silu28 high19 silu29 high20 high21 high22
high23 silu30 high24 high25 silu31 high26 outa0 high27 silu32 high28 outa1 high29 silu33 high30 silu34 silu35
high33 outa2 high34 high35"""
DVE_ORDER = """
stats0 stats1 aggr0 aggr1 mom0 mom1 norm0 norm1 adve0 stats2 adve1 aggr2 xl0 adve2 mom2 adve3 stats3 adve4 v0
adve5 aggr3 adve6 stats4 adve7 mom3 adve8 wl4 adve9 aggr4 v1 mom4 norm3 xl1 norm4 v2 xl2 v3 xl3 wl7 v4 v5 zprep0
v6 soft0 route0 soft1 route1 soft2 route16 soft3 v7 route3 v8 route4 v9 v10 route5 v11 soft4 route6 soft5 v12
route8 route17 route9 v13 route10 route19 route12 route20 v14 route14 route21 route15 v15 route22 v16 route24
v17 route25 route26 h0 route28 v18 h1 route30 v19 h2 route31 v20 h3 low2 h4 v21 high4 h5 low4 h6 cumprod0 db0 h7
cumprod1 h8 rec0 h9 v22 db1 h10 v23 h11 rec1 h12 high11 rec2 h13 v24 high13 h14 v25 high14 h15 v26 h16 rec3 h17
rec4 h18 cumsum0 v27 h19 tail0 h20 tail1 v28 h22 v29 h24 rec5 h25 rec6 h26 rec7 v30 h27 low25 cumsum1 h28 v31
tail2 h30 low27 v32 h31 tail3 high31 v33 h32 v34 h33 high32 v35 h35 low33 low34 low35 out3"""
POOL_ORDER = """
rstd0 rstd1 wl0 wl1 wl3 rstd2 wl2 norm2 rstd3 wl8 rstd4 wl5 wl6 wl9 wl10 route2 wl12 wl11 route7 route18 route23
low0 low1 low3 low5 low6 cteps0 low7 cteps1 low8 low9 low10 low11 low12 low13 low14 low15 z0 low16 low17 low18
low19 low20 low21 low22 low23 low24 z1 out0 low26 out1 low28 low29 low30 low31 low32 out2"""


THIRD = (8, 11, 13, 16)


def items(text):
    return [(x.rstrip("0123456789"), int(x[len(x.rstrip("0123456789")):])) for x in text.split()]


def has(order, what, n):
    return (what, n) in items(order)


def count(order, what, n):
    done = items(order)
    return sum(kind == what for kind, _ in done[:done.index((what, n)) + 1])


def slot(n):
    return 2 if n in THIRD else sum(m not in THIRD for m in range(n)) % 2


def before(n):
    return max((m for m in range(n) if slot(m) == slot(n)), default=None)


def build(nc, x_rows, x_cols, weights, vectors, sel, ident, out):
    with ExitStack() as ctx:
        def sb(name, shape, dt=F32):
            return ctx.enter_context(nc.sbuf_tensor(name, shape, dt))

        def sem(name):
            return ctx.enter_context(nc.semaphore(name))

        xr = sb("xr", [P, BLOCKS, D])
        xt = sb("xt", [P, BATCH * SEQ])
        w = sb("w", [P, C_END])
        wh = sb("wh", [P, C_END], F32R)
        wl = sb("wl", [P, C_END], F32R)
        vec = sb("vec", [P, V_END])
        sels = sb("sels", [KSEL, SELECTORS, P], BF16)
        idf = sb("idf", [P, P])
        idb = sb("idb", [P, P], BF16)
        stats = sb("stats", [P, BLOCKS, 6])
        moments = sb("moments", [P, BLOCKS, 2])
        var_eps = sb("var_eps", [P, BLOCKS])
        neg_mean = sb("neg_mean", [P, BLOCKS])
        minus_half = sb("minus_half", [P, SUB])
        rstd = sb("rstd", [P, BLOCKS])
        shift = sb("shift", [P, BLOCKS])
        xh = sb("xh", [P, BATCH * SEQ], F32R)
        xl = sb("xl", [P, BATCH * SEQ], F32R)
        zb = sb("zb", [P, BLOCKS])
        zneg = sb("zneg", [P, BLOCKS])
        zexp = sb("zexp", [P, BLOCKS])
        zexp1 = sb("zexp1", [P, BLOCKS])
        zexp1_rec = sb("zexp1_rec", [P, BLOCKS])
        zlost = sb("zlost", [P, BLOCKS])
        zfix = sb("zfix", [P, BLOCKS])
        zln = sb("zln", [P, BLOCKS])
        zlog1p = sb("zlog1p", [P, BLOCKS])
        aabs = sb("aabs", [P, 1])
        aexp = sb("aexp", [P, 1])
        aexp1 = sb("aexp1", [P, 1])
        aexp1_rec = sb("aexp1_rec", [P, 1])
        alost = sb("alost", [P, 1])
        afix = sb("afix", [P, 1])
        aln = sb("aln", [P, 1])
        alog1p = sb("alog1p", [P, 1])
        asoft = sb("asoft", [P, 1])
        a_neg = sb("a_neg", [P, 1])
        a_eps = sb("a_eps", [P, 1])
        a_rec = sb("a_rec", [P, 1])
        bias_rec = sb("bias_rec", [P, 1])
        logits_t = sb("logits_t", [ROUTE, BATCH * SEQ])
        lexp = sb("lexp", [P, BLOCKS, EXPERTS])
        lexp1 = sb("lexp1", [P, BLOCKS, EXPERTS])
        scores = sb("scores", [P, BLOCKS, EXPERTS])
        biased = sb("biased", [P, BLOCKS, WIDE])
        top8 = sb("top8", [P, BLOCKS, 8])
        marked = sb("marked", [P, BLOCKS, WIDE])
        chosen = sb("chosen", [P, BLOCKS, EXPERTS])
        picked = sb("picked", [P, BLOCKS, EXPERTS])
        total = sb("total", [P, BLOCKS])
        total_rec = sb("total_rec", [P, BLOCKS])
        routed = sb("routed", [P, BLOCKS, ROW])
        rest1 = sb("rest1", [P, BLOCKS, ROW])
        rest2 = sb("rest2", [P, BLOCKS, ROW])
        routed16 = sb("routed16", [P, BLOCKS, PARTS, ROW], BF16)
        routed_t = sb("routed_t", [KSEL, BATCH * SEQ], BF16)
        silu = sb("silu", [P, SILU_BUFS, TILE])
        v = sb("v", [P, V_BUFS, TILE])
        h = sb("h", [P, H_BUFS, TILE])
        hh = sb("hh", [P, SPLIT_BUFS, TILE], F32R)
        hl = sb("hl", [P, SPLIT_BUFS, TILE], F32R)
        tail = sb("tail", [P, TILES, TILE])
        sels_in = tail[0:KSEL, 0:3, :].rearrange("k t n -> k (t n)")[:, 0:SELECTORS * P].rearrange(
            "k (s n) -> k s n", s=SELECTORS)
        ones = sb("ones", [P, TILE])
        zeros = sb("zeros", [P, TILE])
        fill = zeros[:].bitcast(BF16)
        da = sb("da", [P, GROUPS, TILE])
        ct = sb("ct", [P, GROUPS, TILE + 1])
        ct_eps = sb("ct_eps", [P, GROUPS, TILE])
        ct_rec = sb("ct_rec", [P, GROUPS, TILE])
        bs = sb("bs", [P, GROUPS, TILE])
        db = sb("db", [P, GROUPS, TILE])
        z, s = ct_eps, da
        y_bo = ct_rec[:, 0, :]

        def bank(name):
            return ctx.enter_context(nc.psum_tensor(name, [P, TILE], F32))

        cast_ps, misc_ps, y0, y1 = bank("cast"), bank("misc"), bank("y0"), bank("y1")
        gate_ps = [bank("gate0"), bank("gate1"), cast_ps]
        up_ps = [bank("up0"), bank("up1"), misc_ps]
        y_ps = [[(y0, 0, TILE)], [(y1, 0, TILE)], [(misc_ps, 0, TILE)], [(y0, 0, TILE // 2), (y1, TILE // 2, TILE)]]
        turn_ps = [y0, y1, y0, y1]
        proj_ps = [misc_ps, cast_ps, misc_ps, cast_ps]
        logits = y0[:, 0:BLOCKS * ROUTE].rearrange("p (q r) -> p q r", r=ROUTE)
        spread_ps = [y1, misc_ps]
        pair_ps = [y1, misc_ps]

        consts_done = sem("consts_done")
        x_in = [sem(f"x_in{b}") for b in range(TILES)]
        w_in = [sem(f"w_in{n}") for n in range(len(LOADS))]
        vec_in = sem("vec_in")
        sel_in = sem("sel_in")
        ident_in = sem("ident_in")
        xt_in = sem("xt_in")
        filled = sem("filled")
        stats_done = sem("stats_done")
        aggr_done = sem("aggr_done")
        var_done = sem("var_done")
        rstd_done = sem("rstd_done")
        norm_done = [sem(f"norm_done{c}") for c in range(len(CHUNKS))]
        turned = sem("turned")
        xh_done = sem("xh_done")
        xl_done = sem("xl_done")
        wh_done = sem("wh_done")
        wl_pool = sem("wl_pool")
        wl_dve = sem("wl_dve")
        logits_done = sem("logits_done")
        zb_done = sem("zb_done")
        exp_done = sem("exp_done")
        act_step = sem("act_step")
        route_step = [sem(f"route_step{m}") for m in range(2)]
        soft_step = sem("soft_step")
        aexp_done = sem("aexp_done")
        a_step = sem("a_step")
        spread_done = sem("spread_done")
        routed_t_done = sem("routed_t_done")
        delta_done = sem("delta_done")
        da_done = sem("da_done")
        proj_done = sem("proj_done")
        bs_done = sem("bs_done")
        logits_t_done = sem("logits_t_done")
        ct_done = sem("ct_done")
        ct_eps_done = sem("ct_eps_done")
        square_done = sem("square_done")
        db_done = sem("db_done")
        rec_done = sem("rec_done")
        z_done = sem("z_done")
        s_done = sem("s_done")
        attn_done = [sem(f"attn_done{b}") for b in range(TILES)]
        gate_done = sem("gate_done")
        up_done = sem("up_done")
        silu_done = sem("silu_done")
        v_done = sem("v_done")
        cast_done = sem("cast_done")
        h_done = sem("h_done")
        high_act = sem("high_act")
        high_dve = sem("high_dve")
        low_pool = sem("low_pool")
        low_dve = sem("low_dve")
        down_done = sem("down_done")
        outa_done = sem("outa_done")
        y_done = sem("y_done")
        y_last = sem("y_last")
        y_out = [sem(f"y_out{n}") for n in range(len(OUTS))]

        block = ctx.enter_context(nc.Block())

        def wait_weights(eng, column):
            p = piece_of(column)
            if has(POOL_ORDER, "wl", p):
                eng.wait_ge(wl_pool, count(POOL_ORDER, "wl", p))
            else:
                eng.wait_ge(wl_dve, count(DVE_ORDER, "wl", p))

        def wait_high(eng, n):
            if has(ACT_ORDER, "high", n):
                eng.wait_ge(high_act, count(ACT_ORDER, "high", n))
            else:
                eng.wait_ge(high_dve, count(DVE_ORDER, "high", n))

        def wait_low(eng, n):
            if has(POOL_ORDER, "low", n):
                eng.wait_ge(low_pool, count(POOL_ORDER, "low", n))
            else:
                eng.wait_ge(low_dve, count(DVE_ORDER, "low", n))

        def hidden(n):
            b, e = DOWNS[n]
            return h[:, (b * PAIRS + e) % H_BUFS, :] if e < PAIRS else tail[:, b, :]

        def cols(b):
            return slice(b * TILE, (b + 1) * TILE)

        def shared_half(b):
            return slice(64, 128) if b % 2 == 0 else slice(0, 64)

        def attn_half(b):
            return slice(0, 64) if b % 2 == 0 else slice(64, 128)

        @block.sync
        def _(sp):
            def load_x(b):
                sp.dma_start(xr[:, b * SUB:(b + 1) * SUB, :], x_rows[:, b * SUB:(b + 1) * SUB, :]).then_inc(x_in[b], 16)

            def load_w(n):
                a, b = LOADS[n]
                sp.dma_start(w[:, a:b], weights[:, a:b]).then_inc(w_in[n], 16)

            load_x(0)
            sp.dma_start(vec[:], vectors).then_inc(vec_in, 16)
            load_w(0)
            load_x(1)
            sp.dma_start(idf[:], ident).then_inc(ident_in, 16)
            load_x(2)
            load_w(1)
            load_x(3)
            load_w(2)
            sp.dma_start(sels_in, sel).then_inc(sel_in, 16)
            load_w(3)
            sp.dma_start(xt[:], x_cols).then_inc(xt_in, 16)
            for n, (a, b) in enumerate(OUTS):
                if n < TILES - 1:
                    sp.wait_ge(y_done, n + 1)
                else:
                    sp.wait_ge(y_last, n - TILES + 2)
                sp.dma_start(out[:, a:b], xt[:, a:b]).then_inc(y_out[n], 16)
            for n in range(len(OUTS)):
                sp.wait_ge(y_out[n], 16)

        @block.gpsimd
        def _(pool):
            pool.memset(minus_half[:], -0.5).then_inc(filled, 1)
            pool.memset(zeros[:], 0.0).then_inc(filled, 1)
            pool.memset(ones[:], 1.0).then_inc(filled, 1)
            pool.memset(ct[:, :, 0:1], 1.0).then_inc(filled, 1)
            pool.memset(biased[:, :, EXPERTS:WIDE], FILLER).then_inc(filled, 1)
            pool.wait_ge(filled, 5)
            for what, n in items(POOL_ORDER):
                if what == "rstd":
                    a, b = CHUNKS[n]
                    pool.wait_ge(var_done, n + 1)
                    pool.tensor_tensor(rstd[:, a:b], var_eps[:, a:b], minus_half[:, 0:b - a],
                                       ALU.pow).then_inc(rstd_done, 1)
                if what == "norm":
                    pool.wait_ge(rstd_done, n + 1)
                    for q in range(*CHUNKS[n]):
                        last = pool.tensor_scalar(xr[:, q, :], xr[:, q, :], neg_mean[:, q:q + 1], rstd[:, q:q + 1],
                                                  ALU.add, ALU.mult)
                    last.then_inc(norm_done[n], 1)
                if what == "route":
                    m, k = divmod(n, ROUTE_STEPS)
                    q = slice(m * HALF, (m + 1) * HALF)
                    pool.wait_ge(route_step[m], k)
                    if k == 2:
                        last = pool.tensor_tensor(biased[:, q, 0:EXPERTS], scores[:, q, :],
                                                  vec[:, None, V_GB:V_END].to_broadcast([P, HALF, EXPERTS]), ALU.add)
                    if k == 7:
                        last = pool.tensor_tensor(picked[:, q, :], scores[:, q, :], chosen[:, q, :], ALU.mult)
                    last.then_inc(route_step[m], 1)
                if what == "wl":
                    a, b = PIECES[n]
                    pool.wait_ge(wh_done, count(ACT_ORDER, "wh", n))
                    pool.tensor_tensor(wl[:, a:b], w[:, a:b], wh[:, a:b].bitcast(F32),
                                       ALU.subtract).then_inc(wl_pool, 1)
                if what == "cteps":
                    pool.wait_ge(ct_done, n + 1)
                    pool.tensor_scalar(ct_eps[:, n, :], ct[:, n, 0:TILE], ATTN_EPS, 1.0, ALU.add,
                                       ALU.mult).then_inc(ct_eps_done, 1)
                if what == "z":
                    pool.wait_ge(rec_done, SUB * (n + 1))
                    pool.wait_ge(db_done, n + 1)
                    pool.tensor_tensor(z[:, n, :], db[:, n, :], ct_rec[:, n, :], ALU.mult).then_inc(z_done, 1)
                if what == "out":
                    pool.wait_ge(xt_in, 16)
                    pool.wait_ge(outa_done, n + 1)
                    pool.tensor_tensor(xt[:, cols(n)], y_bo[:], xt[:, cols(n)], ALU.add).then_inc(y_done, 1)
                if what == "low":
                    wait_high(pool, n)
                    if n >= SPLIT_BUFS:
                        pool.wait_ge(down_done, n - SPLIT_BUFS + 1)
                    pool.tensor_tensor(hl[:, n % SPLIT_BUFS, :], hidden(n), hh[:, n % SPLIT_BUFS, :].bitcast(F32),
                                       ALU.subtract).then_inc(low_pool, 1)

        @block.scalar
        def _(act):
            steps = [0]

            def link(ins):
                steps[0] += 1
                ins.then_inc(act_step, 1)
                act.wait_ge(act_step, steps[0])

            for what, n in items(ACT_ORDER):
                if what == "table":
                    act.preload_act_table_set("silu_and_others" if n % 2 else "natural_log_exp_and_others")
                if what == "acalc":
                    act.wait_ge(vec_in, 16)
                    link(act.activation(aabs[:], vec[:, V_ALOG:V_ALOG + 1], ACT.Abs))
                    link(act.activation(aexp[:], aabs[:], ACT.Exp, scale=-1.0))
                    act.activation(aln[:], aexp[:], ACT.Ln, bias=1.0).then_inc(aexp_done, 1)
                if what == "wh":
                    a, b = PIECES[n]
                    act.wait_ge(w_in[load_of(n)], 16)
                    act.activation(wh[:, a:b], w[:, a:b], ACT.Copy).then_inc(wh_done, 1)
                if what == "consts":
                    act.wait_ge(sel_in, 16)
                    act.wait_ge(ident_in, 16)
                    act.activation(sels[:], sels_in, ACT.Copy).then_inc(consts_done, 1)
                    act.activation(idb[:], idf[:], ACT.Copy).then_inc(consts_done, 1)
                if what == "xh":
                    act.wait_ge(turned, n + 1)
                    act.activation(xh[:, cols(n)], turn_ps[n][:], ACT.Copy).then_inc(xh_done, 1)
                if what == "bs":
                    act.wait_ge(proj_done, n + 1)
                    act.wait_ge(a_step, 10)
                    half, other = attn_half(n), shared_half(n)
                    act.activation(logits_t[:, cols(n)], proj_ps[n][other.start:other.start + ROUTE, :],
                                   ACT.Copy).then_inc(logits_t_done, 1)
                    act.activation(bs[half, n // 2, :], proj_ps[n][half, :], ACT.Identity, bias=bias_rec[half, 0:1],
                                   scale=a_rec[half, 0:1]).then_inc(bs_done, 1)
                if what == "sig":
                    act.wait_ge(zb_done, 1)
                    act.activation(lexp[:], logits[:, :, 0:EXPERTS], ACT.Exp, scale=-1.0).then_inc(exp_done, 1)
                    act.wait_ge(zb_done, 2)
                    link(act.activation(zexp[:], zneg[:], ACT.Exp))
                    act.activation(zln[:], zexp[:], ACT.Ln, bias=1.0).then_inc(exp_done, 1)
                if what == "route":
                    m, k = divmod(n, ROUTE_STEPS)
                    q = slice(m * HALF, (m + 1) * HALF)
                    act.wait_ge(route_step[m], k)
                    if k == 11:
                        act.wait_ge(soft_step, 6)
                        last = act.activation(routed16[:, q, 0, :], routed[:, q, :], ACT.Copy)
                    if k == 13:
                        last = act.activation(routed16[:, q, 1, :], rest1[:, q, :], ACT.Copy)
                    last.then_inc(route_step[m], 1)
                if what == "routedt":
                    act.wait_ge(spread_done, n + 1)
                    act.activation(routed_t[:, 2 * n * TILE:(2 * n + 2) * TILE],
                                   spread_ps[n][:].bitcast(BF16)[0:KSEL, :], ACT.Copy).then_inc(routed_t_done, 1)
                if what == "decay":
                    act.wait_ge(a_step, 10)
                    act.wait_ge(delta_done, n + 1)
                    act.activation(da[:, n, :], pair_ps[n][:], ACT.Exp, scale=a_neg[:, 0:1]).then_inc(da_done, 1)
                if what == "square":
                    act.wait_ge(ct_eps_done, n + 1)
                    act.activation(ct[:, n, 0:TILE], ct[:, n, 0:TILE], ACT.Square).then_inc(square_done, 1)
                if what == "outa":
                    act.wait_ge(vec_in, 16)
                    act.wait_ge(down_done, LAST_OF[n] + 1)
                    act.wait_ge(z_done, 1)
                    if n:
                        act.wait_ge(y_done, n)
                    act.activation(y_bo[:], y_ps[n][0][0][:], ACT.Identity,
                                   bias=vec[:, V_BO:V_BO + 1]).then_inc(outa_done, 1)
                if what == "silu":
                    b, e = divmod(n, STEPS)
                    act.wait_ge(gate_done, n + 1)
                    if n >= SILU_BUFS:
                        act.wait_ge(v_done, n - SILU_BUFS + 1)
                    if e < PAIRS:
                        act.activation(silu[:, n % SILU_BUFS, :], gate_ps[slot(n)][:], ACT.Silu).then_inc(silu_done, 1)
                    else:
                        act.activation(silu[shared_half(b), n % SILU_BUFS, :], gate_ps[slot(n)][attn_half(b), :],
                                       ACT.Silu).then_inc(silu_done, 1)
                if what == "high":
                    b, e = DOWNS[n]
                    if e < PAIRS:
                        act.wait_ge(h_done, b * PAIRS + e + 1)
                    else:
                        act.wait_ge(v_done, b * STEPS + STEPS)
                        act.wait_ge(attn_done[b], 1)
                    if n >= SPLIT_BUFS:
                        act.wait_ge(down_done, n - SPLIT_BUFS + 1)
                    act.activation(hh[:, n % SPLIT_BUFS, :], hidden(n), ACT.Copy).then_inc(high_act, 1)

        @block.vector
        def _(dve):
            for what, n in items(DVE_ORDER):
                if what == "stats":
                    dve.wait_ge(x_in[CHUNKS[n][0] // SUB], 16)
                    for q in range(*CHUNKS[n]):
                        last = dve.bn_stats(stats[:, q, :], xr[:, q, :])
                    last.then_inc(stats_done, 1)
                if what == "aggr":
                    dve.wait_ge(stats_done, n + 1)
                    for q in range(*CHUNKS[n]):
                        last = dve.bn_aggr(moments[:, q, :], stats[:, q, :])
                    last.then_inc(aggr_done, 1)
                if what == "mom":
                    a, b = CHUNKS[n]
                    dve.wait_ge(aggr_done, n + 1)
                    dve.tensor_scalar(neg_mean[:, a:b], moments[:, a:b, 0], -1.0, None, ALU.mult)
                    dve.tensor_scalar(var_eps[:, a:b], moments[:, a:b, 1], LN_EPS, None,
                                      ALU.add).then_inc(var_done, 1)
                if what == "adve":
                    if n == 0:
                        dve.wait_ge(aexp_done, 1)
                        dve.wait_ge(vec_in, 16)
                        last = dve.tensor_scalar(aexp1[:], aexp[:], 1.0, None, ALU.add)
                    else:
                        dve.wait_ge(a_step, n)
                    if n == 1:
                        last = dve.scalar_tensor_tensor(out=alost[:], in0=aexp1[:], scalar=1.0, in1=aexp[:],
                                                        op0=ALU.subtract, op1=ALU.subtract)
                    if n == 2:
                        last = dve.reciprocal(aexp1_rec[:], aexp1[:])
                    if n == 3:
                        last = dve.tensor_tensor(afix[:], alost[:], aexp1_rec[:], ALU.mult)
                    if n == 4:
                        last = dve.tensor_tensor(alog1p[:], aln[:], afix[:], ALU.subtract)
                    if n == 5:
                        last = dve.scalar_tensor_tensor(out=asoft[:], in0=vec[:, V_ALOG:V_ALOG + 1], scalar=0.0,
                                                        in1=alog1p[:], op0=ALU.max, op1=ALU.add)
                    if n == 6:
                        last = dve.tensor_scalar(a_neg[:], asoft[:], -1.0, None, ALU.mult)
                    if n == 7:
                        last = dve.tensor_scalar(a_eps[:], a_neg[:], ATTN_EPS, None, ALU.add)
                    if n == 8:
                        last = dve.reciprocal(a_rec[:], a_eps[:])
                    if n == 9:
                        last = dve.tensor_tensor(bias_rec[:], vec[:, V_BB:V_BB + 1], a_rec[:], ALU.mult)
                    last.then_inc(a_step, 1)
                if what == "norm":
                    dve.wait_ge(rstd_done, n + 1)
                    dve.wait_ge(var_done, n + 1)
                    for q in range(*CHUNKS[n]):
                        last = dve.tensor_scalar(xr[:, q, :], xr[:, q, :], neg_mean[:, q:q + 1],
                                                 rstd[:, q:q + 1], ALU.add, ALU.mult)
                    last.then_inc(norm_done[n], 1)
                if what == "wl":
                    a, b = PIECES[n]
                    dve.wait_ge(wh_done, count(ACT_ORDER, "wh", n))
                    dve.tensor_tensor(wl[:, a:b], w[:, a:b], wh[:, a:b].bitcast(F32), ALU.subtract).then_inc(wl_dve, 1)
                if what == "xl":
                    dve.wait_ge(xh_done, n + 1)
                    dve.tensor_tensor(xl[:, cols(n)], turn_ps[n][:], xh[:, cols(n)].bitcast(F32),
                                      ALU.subtract).then_inc(xl_done, 1)
                if what == "zprep":
                    dve.wait_ge(vec_in, 16)
                    dve.wait_ge(logits_done, 1)
                    dve.tensor_scalar(zb[:], logits[:, :, EXPERTS], vec[:, V_BD:V_BD + 1], None,
                                      ALU.add).then_inc(zb_done, 1)
                    dve.wait_ge(zb_done, 1)
                    dve.scalar_tensor_tensor(out=zneg[:], in0=zb[:], scalar=-1.0, in1=zb[:], op0=ALU.mult,
                                             op1=ALU.min).then_inc(zb_done, 1)
                if what == "route":
                    m, k = divmod(n, ROUTE_STEPS)
                    q = slice(m * HALF, (m + 1) * HALF)
                    if k > 0:
                        dve.wait_ge(route_step[m], k)
                    if k == 0:
                        dve.wait_ge(exp_done, 1)
                        last = dve.tensor_scalar(lexp1[:, q, :], lexp[:, q, :], 1.0, None, ALU.add)
                    if k == 1:
                        last = dve.reciprocal(scores[:, q, :], lexp1[:, q, :])
                    if k == 3:
                        for j in range(m * HALF, (m + 1) * HALF):
                            last = dve.max(top8[:, j, :], biased[:, j, 0:EXPERTS])
                    if k == 4:
                        last = dve.memset(top8[:, q, TOPK:8], FILLER)
                    if k == 5:
                        for j in range(m * HALF, (m + 1) * HALF):
                            last = dve.match_replace(marked[:, j, :], top8[:, j, :], biased[:, j, :], TAKEN)
                    if k == 6:
                        last = dve.tensor_tensor(chosen[:, q, :], marked[:, q, 0:EXPERTS], biased[:, q, 0:EXPERTS],
                                                 ALU.not_equal)
                    if k == 8:
                        last = dve.tensor_reduce(total[:, q], picked[:, q, :], AX_X, ALU.add)
                    if k == 9:
                        last = dve.reciprocal(total_rec[:, q], total[:, q])
                    if k == 10:
                        last = dve.scalar_tensor_tensor(
                            out=routed[:, q, 0:EXPERTS], in0=picked[:, q, :], scalar=ROUTE_SCALE,
                            in1=total_rec[:, q, None].to_broadcast([P, HALF, EXPERTS]), op0=ALU.mult, op1=ALU.mult)
                    if k == 12:
                        last = dve.tensor_tensor(rest1[:, q, :], routed[:, q, :], routed16[:, q, 0, :], ALU.subtract)
                    if k == 14:
                        last = dve.tensor_tensor(rest2[:, q, :], rest1[:, q, :], routed16[:, q, 1, :], ALU.subtract)
                    if k == 15:
                        last = dve.tensor_copy(routed16[:, q, 2, :], rest2[:, q, :])
                    last.then_inc(route_step[m], 1)
                if what == "soft":
                    if n == 0:
                        dve.wait_ge(exp_done, 2)
                        last = dve.tensor_scalar(zexp1[:], zexp[:], 1.0, None, ALU.add)
                    else:
                        dve.wait_ge(soft_step, n)
                    if n == 1:
                        last = dve.scalar_tensor_tensor(out=zlost[:], in0=zexp1[:], scalar=1.0, in1=zexp[:],
                                                        op0=ALU.subtract, op1=ALU.subtract)
                    if n == 2:
                        last = dve.reciprocal(zexp1_rec[:], zexp1[:])
                    if n == 3:
                        last = dve.tensor_tensor(zfix[:], zlost[:], zexp1_rec[:], ALU.mult)
                    if n == 4:
                        last = dve.tensor_tensor(zlog1p[:], zln[:], zfix[:], ALU.subtract)
                    if n == 5:
                        last = dve.scalar_tensor_tensor(out=routed[:, :, EXPERTS], in0=zb[:], scalar=0.0,
                                                        in1=zlog1p[:], op0=ALU.max, op1=ALU.add)
                    last.then_inc(soft_step, 1)
                if what == "cumprod":
                    dve.wait_ge(da_done, n + 1)
                    dve.tensor_tensor_scan(ct[:, n, 1:TILE + 1], da[:, n, :], zeros[:], 1.0, ALU.mult,
                                           ALU.add).then_inc(ct_done, 1)
                if what == "db":
                    dve.wait_ge(da_done, n + 1)
                    dve.wait_ge(bs_done, 2 * (n + 1))
                    dve.scalar_tensor_tensor(out=db[:, n, :], in0=da[:, n, :], scalar=1.0, in1=bs[:, n, :],
                                             op0=ALU.subtract, op1=ALU.mult).then_inc(db_done, 1)
                if what == "rec":
                    g, part = divmod(n, SUB)
                    c = slice(part * P, (part + 1) * P)
                    dve.wait_ge(ct_eps_done, g + 1)
                    dve.reciprocal(ct_rec[:, g, c], ct_eps[:, g, c]).then_inc(rec_done, 1)
                if what == "cumsum":
                    dve.wait_ge(z_done, n + 1)
                    dve.tensor_tensor_scan(s[:, n, :], ones[:], z[:, n, :], 0.0, ALU.mult,
                                           ALU.add).then_inc(s_done, 1)
                if what == "tail":
                    half, g = attn_half(n), n // 2
                    dve.wait_ge(s_done, g + 1)
                    dve.wait_ge(square_done, g + 1)
                    dve.wait_ge(consts_done, 1)
                    dve.tensor_tensor(tail[half, n, :], ct[half, g, 0:TILE], s[half, g, :],
                                      ALU.mult).then_inc(attn_done[n], 1)
                if what == "v":
                    b, e = divmod(n, STEPS)
                    dve.wait_ge(silu_done, n + 1)
                    if e < PAIRS:
                        i = b * PAIRS + e
                        dve.wait_ge(up_done, i + 1)
                        if i >= V_BUFS:
                            dve.wait_ge(h_done, i - V_BUFS + 1)
                        dve.tensor_tensor(v[:, i % V_BUFS, :], silu[:, n % SILU_BUFS, :], up_ps[slot(n)][:],
                                          ALU.mult).then_inc(v_done, 1)
                    else:
                        half = shared_half(b)
                        dve.wait_ge(consts_done, 1)
                        dve.tensor_tensor(tail[half, b, :], silu[half, n % SILU_BUFS, :], gate_ps[slot(n)][half, :],
                                          ALU.mult).then_inc(v_done, 1)
                if what == "h":
                    b, e = DOWNS[n]
                    i = b * PAIRS + e
                    dve.wait_ge(cast_done, i + 1)
                    dve.wait_ge(v_done, b * STEPS + e + 1)
                    if i >= H_BUFS:
                        wait_low(dve, DOWNS.index(divmod(i - H_BUFS, PAIRS)))
                    dve.tensor_tensor(h[:, i % H_BUFS, :], v[:, i % V_BUFS, :], cast_ps[:],
                                      ALU.mult).then_inc(h_done, 1)
                if what == "high":
                    b, e = DOWNS[n]
                    if e < PAIRS:
                        dve.wait_ge(h_done, b * PAIRS + e + 1)
                    else:
                        dve.wait_ge(v_done, b * STEPS + STEPS)
                        dve.wait_ge(attn_done[b], 1)
                    if n >= SPLIT_BUFS:
                        dve.wait_ge(down_done, n - SPLIT_BUFS + 1)
                    dve.tensor_copy(hh[:, n % SPLIT_BUFS, :], hidden(n)).then_inc(high_dve, 1)
                if what == "low":
                    wait_high(dve, n)
                    if n >= SPLIT_BUFS:
                        dve.wait_ge(down_done, n - SPLIT_BUFS + 1)
                    dve.tensor_tensor(hl[:, n % SPLIT_BUFS, :], hidden(n), hh[:, n % SPLIT_BUFS, :].bitcast(F32),
                                      ALU.subtract).then_inc(low_dve, 1)
                if what == "out":
                    dve.wait_ge(xt_in, 16)
                    for part, (a, b) in enumerate(OUTS[n:]):
                        dve.wait_ge(down_done, LAST_OF[n] + 1 + part)
                        bank_ps, x, y = y_ps[n][part]
                        dve.scalar_tensor_tensor(out=xt[:, a:b], in0=bank_ps[:, x:y],
                                                 scalar=vec[:, V_BO:V_BO + 1], in1=xt[:, a:b], op0=ALU.add,
                                                 op1=ALU.add).then_inc(y_last, 1)

        @block.tensor
        def _(pe):
            def product(dst, column, high, low, first=True, last=True, low_of=None):
                pe.matmul(dst, wh[:, column:column + P], high, start=first, stop=False)
                pe.matmul(dst, wl[:, column:column + P], high, start=False, stop=False)
                if low_of is not None:
                    pe.wait_ge(xl_done, low_of + 1)
                return pe.matmul(dst, wh[:, column:column + P], low, start=False, stop=last)

            for what, n in items(PE_ORDER):
                if what == "warm":
                    if n == 0:
                        pe.wait_ge(filled, 2)
                    for _ in range(WARM[n]):
                        pe.matmul(misc_ps[:], fill[:, 0:P], fill[:, 0:TILE], start=True, stop=True)
                if what == "turn":
                    if n == 0:
                        pe.wait_ge(ident_in, 16)
                    if n >= 2:
                        pe.wait_ge(xl_done, n - 1)
                    for q in range(SUB):
                        for c, (a, b) in enumerate(CHUNKS):
                            if a == n * SUB + q:
                                pe.wait_ge(norm_done[c], 1)
                        last = pe.transpose(turn_ps[n][:, q * P:(q + 1) * P], xr[:, n * SUB + q, :], idf[:])
                    last.then_inc(turned, 1)
                if what == "proj":
                    pe.wait_ge(xh_done, n + 1)
                    wait_weights(pe, C_PROJ)
                    if n >= 2:
                        pe.wait_ge(bs_done, n - 1)
                    product(proj_ps[n][:], C_PROJ + P * (n % 2), xh[:, cols(n)], xl[:, cols(n)],
                            low_of=n).then_inc(proj_done, 1)
                if what == "logits":
                    pe.wait_ge(xl_done, 3)
                    for b in range(TILES):
                        pe.wait_ge(logits_t_done, b + 1)
                        for q in range(b * SUB, (b + 1) * SUB):
                            last = pe.transpose(logits[:, q, :], logits_t[:, q * P:(q + 1) * P],
                                                idf[0:ROUTE, 0:ROUTE])
                    last.then_inc(logits_done, 1)
                if what == "spread":
                    if n == 0:
                        pe.wait_ge(consts_done, 2)
                    pe.wait_ge(route_step[n], ROUTE_STEPS)
                    pe.wait_ge(xl_done, 4)
                    if n == 1:
                        pe.wait_ge(bs_done, 3)
                        if THIRD:
                            pe.wait_ge(v_done, max(THIRD) + 1)
                    for q in range(BLOCKS // 2):
                        last = pe.transpose(spread_ps[n][:].bitcast(BF16)[0:KSEL, q * P:(q + 1) * P],
                                            routed16[:, n * BLOCKS // 2 + q, :, :].rearrange("p a r -> p (a r)"),
                                            idb[:])
                    last.then_inc(spread_done, 1)
                if what == "delta":
                    pe.wait_ge(routed_t_done, n + 1)
                    pe.matmul(pair_ps[n][:], sels[:, PAIRS, :], routed_t[:, cols(2 * n)], start=True, stop=False)
                    pe.matmul(pair_ps[n][:], sels[:, PAIRS + 1, :], routed_t[:, cols(2 * n + 1)], start=False,
                              stop=True).then_inc(delta_done, 1)
                if what == "gate":
                    b, e = divmod(n, STEPS)
                    column = up_column(e) if e < PAIRS else C_SHARED + (b % 2) * P
                    if e == 0:
                        pe.wait_ge(xh_done, b + 1)
                    if b == 0:
                        wait_weights(pe, column)
                    if before(n) is not None:
                        pe.wait_ge(v_done, before(n) + 1)
                    if n in THIRD:
                        pe.wait_ge(bs_done, TILES)
                    product(gate_ps[slot(n)][:], column, xh[:, cols(b)], xl[:, cols(b)],
                            low_of=b if e == 0 else None).then_inc(gate_done, 1)
                if what == "up":
                    b, e = divmod(n, STEPS)
                    product(up_ps[slot(n)][:], up_column(e) + P, xh[:, cols(b)], xl[:, cols(b)]).then_inc(
                        up_done, 1)
                if what == "cast":
                    b, e = DOWNS[n]
                    i = b * PAIRS + e
                    if e == 0:
                        pe.wait_ge(routed_t_done, b // 2 + 1)
                    if i:
                        pe.wait_ge(h_done, i)
                    else:
                        pe.wait_ge(bs_done, TILES)
                        pe.wait_ge(v_done, max(THIRD) + 1)
                    pe.matmul(cast_ps[:], sels[:, e, :], routed_t[:, cols(b)], start=True,
                              stop=True).then_inc(cast_done, 1)
                if what == "down":
                    b, e = DOWNS[n]
                    wait_low(pe, n)
                    column = C_DOWN + P * e if e < PAIRS else C_TAIL + P * (b % 2)
                    if b == 0 or e == PAIRS:
                        wait_weights(pe, column)
                    if n == FIRST_OF[b]:
                        if b == 0:
                            pe.wait_ge(exp_done, 1)
                        if b == 1:
                            pe.wait_ge(da_done, 1)
                        if b == 2:
                            pe.wait_ge(da_done, 2)
                        if b == 3:
                            pe.wait_ge(outa_done, 2)
                    for bank_ps, x, y in y_ps[b]:
                        last = product(bank_ps[:, x:y], column, hh[:, n % SPLIT_BUFS, x:y], hl[:, n % SPLIT_BUFS, x:y],
                                       first=n == FIRST_OF[b], last=n == LAST_OF[b])
                        if n == LAST_OF[b] or y == TILE:
                            last.then_inc(down_done, 1)


def layouts(a):
    x = a["L0_attn_x"].reshape(BATCH * SEQ, D)
    w13, w2 = a["L0_ffn_w13"], a["L0_ffn_w2"]
    gate_up = w13.reshape(PAIRS, 2, 2, INTER, D).transpose(4, 0, 2, 1, 3).reshape(D, PAIRS * 256)
    down = w2.reshape(PAIRS, 2, D, INTER).transpose(1, 3, 0, 2).reshape(P, PAIRS * D)
    gate_s, up_s = a["L0_ffn_w13_s"][:INTER].T, a["L0_ffn_w13_s"][INTER:].T
    wb, wo, w2_s, wd = a["L0_attn_WB"].T, a["L0_attn_Wo"].T, a["L0_ffn_w2_s"].T, a["L0_attn_Wd"].T
    route = np.concatenate([a["L0_ffn_gate_w"].T, wd, np.zeros((D, STATES - ROUTE), np.float32)], axis=1)
    weights = np.concatenate([
        gate_up[:, :C_PROJ], wb, route, route, wb, gate_up[:, C_PROJ:], gate_s, up_s, up_s, gate_s, down,
        np.concatenate([wo, w2_s]), np.concatenate([w2_s, wo])], axis=1)
    vectors = np.concatenate([
        np.tile(a["L0_attn_A_log"], 2)[:, None], np.tile(a["L0_attn_bB"], 2)[:, None], a["L0_attn_bo"][:, None],
        np.tile(a["L0_attn_bd"], P)[:, None], np.tile(a["L0_ffn_gate_b"][None, :], (P, 1))], axis=1)
    sel = np.zeros((KSEL, SELECTORS, P), np.float32)
    for part in range(PARTS):
        for e in range(EXPERTS):
            sel[part * ROW + e, e // 2, (e % 2) * INTER:(e % 2 + 1) * INTER] = 1
        sel[part * ROW + EXPERTS, PAIRS, 0:STATES] = 1
        sel[part * ROW + EXPERTS, PAIRS + 1, STATES:P] = 1
    return {
        "x_rows": x.reshape(BLOCKS, P, D).transpose(1, 0, 2),
        "x_cols": x.T,
        "weights": weights,
        "vectors": vectors,
        "sel": sel,
        "ident": np.eye(P, dtype=np.float32),
    }


def kernel(**inputs):
    import concourse.bacc as bacc
    from concourse.bass_utils import run_bass_kernel_spmd

    arrays = {k: np.ascontiguousarray(v) for k, v in layouts({k: np.asarray(v) for k, v in inputs.items()}).items()}
    nc = bacc.Bacc("TRN2", target_bir_lowering=False, num_devices=1)
    args = [nc.dram_tensor(k, v.shape, mybir.dt.from_np(v.dtype), kind="ExternalInput").ap()
            for k, v in arrays.items()]
    out = nc.dram_tensor("out", (D, BATCH * SEQ), F32, kind="ExternalOutput").ap()
    build(nc, *args, out)
    result = run_bass_kernel_spmd(nc, [arrays], core_ids=[0]).results[0]["out"]
    return np.ascontiguousarray(result.T).reshape(BATCH, SEQ, D)
```
